# Optimizing a Trainium2 kernel written in Bass

```python
import numpy as np
import jax
import jax.numpy as jnp

def _softmax(x, axis=-1):
    return jax.nn.softmax(x, axis=axis)

def _gelu(x):
    return jax.nn.gelu(x, approximate=True)

def _silu(x):
    return jax.nn.silu(x)

def _sigmoid(x):
    return jax.nn.sigmoid(x)

def _layernorm(x, axis=-1, eps=1e-05):
    m = jnp.mean(x, axis=axis, keepdims=True)
    v = jnp.var(x, axis=axis, keepdims=True)
    return (x - m) / jnp.sqrt(v + eps)

def _scatter_add(tgt, idx, src, axis=0):
    return tgt.at[idx].add(src)

def _segment_sum(src, seg, n):
    return jax.ops.segment_sum(src, seg, n)
kernel_name = 'mk_conv_preact_d2_conv_nchw256_r2_3f93f1'

def setup_inputs(seed: int=0):
    np.random.seed(seed)
    _w = jnp.asarray

    def _rec_inputs():
        import jax
        import jax.numpy as jnp
        _gk = jax.random.key(seed)
        x = -0.0005207 + 1.001 * jax.random.normal(jax.random.fold_in(_gk, 1), (2, 128, 32, 32), jnp.float32)
        return x
    x = _rec_inputs()

    def _L0_conv_setup():
        import jax, jax.numpy as jnp
        import numpy as np
        CHANNELS = 128
        HEADS = 8
        HEAD_DIM = CHANNELS // HEADS
        SCALE = HEAD_DIM ** (-0.5)
        key = jax.random.key(seed)
        ks = jax.random.split(key, 9)
        x = jax.random.normal(ks[0], (2, CHANNELS, 32, 32), dtype=jnp.float32)

        def w(k):
            bound = 1.0 / np.sqrt(HEAD_DIM)
            return jax.random.uniform(k, (HEADS, HEAD_DIM, HEAD_DIM), dtype=jnp.float32, minval=-bound, maxval=bound)

        def b(k):
            bound = 1.0 / np.sqrt(HEAD_DIM)
            return jax.random.uniform(k, (HEADS, HEAD_DIM), dtype=jnp.float32, minval=-bound, maxval=bound)
        return {'x': x, 'Wq': w(ks[1]), 'bq': b(ks[2]), 'Wk': w(ks[3]), 'bk': b(ks[4]), 'Wv': w(ks[5]), 'bv': b(ks[6]), 'Wp': w(ks[7]), 'bp': b(ks[8])}
    _L0_conv_all = _L0_conv_setup()
    _L0_conv_in = {k: v for k, v in _L0_conv_all.items() if k in ('Wq', 'bq', 'Wk', 'bk', 'Wv', 'bv', 'Wp', 'bp')}
    del _L0_conv_all

    def _L1_conv_setup():
        import jax, jax.numpy as jnp
        import numpy as np
        from jax import lax
        B, DIM, H, W = (32, 128, 56, 56)
        HID = 4 * DIM
        EPS = 1e-06
        key = jax.random.key(seed)
        ks = jax.random.split(key, 8)
        x = jax.random.normal(ks[0], (B, DIM, H, W), dtype=jnp.float32)
        conv_w = jax.random.normal(ks[1], (DIM, 1, 7, 7), dtype=jnp.float32) * 0.05
        conv_b = jax.random.normal(ks[2], (DIM,), dtype=jnp.float32) * 0.01
        ln_g = jnp.ones((DIM,), dtype=jnp.float32)
        ln_b = jnp.zeros((DIM,), dtype=jnp.float32)
        w1 = jax.random.normal(ks[3], (DIM, HID), dtype=jnp.float32) * (1.0 / np.sqrt(DIM))
        b1 = jax.random.normal(ks[4], (HID,), dtype=jnp.float32) * 0.01
        w2 = jax.random.normal(ks[5], (HID, DIM), dtype=jnp.float32) * (1.0 / np.sqrt(HID))
        b2 = jax.random.normal(ks[6], (DIM,), dtype=jnp.float32) * 0.01
        return {'x': x, 'conv_w': conv_w, 'conv_b': conv_b, 'ln_g': ln_g, 'ln_b': ln_b, 'w1': w1, 'b1': b1, 'w2': w2, 'b2': b2}
    _L1_conv_all = _L1_conv_setup()
    _L1_conv_in = {k: v for k, v in _L1_conv_all.items() if k in ('conv_w', 'conv_b', 'ln_g', 'ln_b', 'w1', 'b1', 'w2', 'b2')}
    del _L1_conv_all
    return {'x': x, 'L0_conv_Wq': _L0_conv_in['Wq'], 'L0_conv_bq': _L0_conv_in['bq'], 'L0_conv_Wk': _L0_conv_in['Wk'], 'L0_conv_bk': _L0_conv_in['bk'], 'L0_conv_Wv': _L0_conv_in['Wv'], 'L0_conv_bv': _L0_conv_in['bv'], 'L0_conv_Wp': _L0_conv_in['Wp'], 'L0_conv_bp': _L0_conv_in['bp'], 'L1_conv_conv_w': _L1_conv_in['conv_w'], 'L1_conv_conv_b': _L1_conv_in['conv_b'], 'L1_conv_ln_g': _L1_conv_in['ln_g'], 'L1_conv_ln_b': _L1_conv_in['ln_b'], 'L1_conv_w1': _L1_conv_in['w1'], 'L1_conv_b1': _L1_conv_in['b1'], 'L1_conv_w2': _L1_conv_in['w2'], 'L1_conv_b2': _L1_conv_in['b2']}

def reference(x, L0_conv_Wq, L0_conv_bq, L0_conv_Wk, L0_conv_bk, L0_conv_Wv, L0_conv_bv, L0_conv_Wp, L0_conv_bp, L1_conv_conv_w, L1_conv_conv_b, L1_conv_ln_g, L1_conv_ln_b, L1_conv_w1, L1_conv_b1, L1_conv_w2, L1_conv_b2):
    import jax
    import jax.numpy as jnp

    def _L0_conv_ref(x, Wq, bq, Wk, bk, Wv, bv, Wp, bp):
        import jax, jax.numpy as jnp
        import numpy as np
        CHANNELS = 128
        HEADS = 8
        HEAD_DIM = CHANNELS // HEADS
        SCALE = HEAD_DIM ** (-0.5)
        b_, c, h, w = x.shape
        n = h * w
        xh = x.reshape(b_, HEADS, HEAD_DIM, n)
        proj = lambda W, bias, t: jnp.einsum('god,bgdn->bgon', W, t) + bias[None, :, :, None]
        q = proj(Wq, bq, xh)
        k = proj(Wk, bk, xh)
        v = proj(Wv, bv, xh)
        attn = jnp.einsum('bgdi,bgdj->bgij', q, k) * SCALE
        attn = jax.nn.softmax(attn, axis=-1)
        out = jnp.einsum('bgij,bgdj->bgdi', attn, v)
        out = proj(Wp, bp, out)
        return out.reshape(b_, c, h, w)

    def _L1_conv_ref(x, conv_w, conv_b, ln_g, ln_b, w1, b1, w2, b2):
        import jax, jax.numpy as jnp
        import numpy as np
        from jax import lax
        B, DIM, H, W = (32, 128, 56, 56)
        HID = 4 * DIM
        EPS = 1e-06
        dim = x.shape[1]
        y = lax.conv_general_dilated(x, conv_w, window_strides=(1, 1), padding=((3, 3), (3, 3)), dimension_numbers=('NCHW', 'OIHW', 'NCHW'), feature_group_count=dim)
        y = y + conv_b[None, :, None, None]
        y = jnp.transpose(y, (0, 2, 3, 1))
        mu = jnp.mean(y, axis=-1, keepdims=True)
        var = jnp.mean(jnp.square(y - mu), axis=-1, keepdims=True)
        y = (y - mu) * lax.rsqrt(var + EPS) * ln_g + ln_b
        h = jax.nn.gelu(jnp.einsum('bhwc,cf->bhwf', y, w1) + b1, approximate=False)
        y = jnp.einsum('bhwf,fc->bhwc', h, w2) + b2
        return jnp.transpose(y, (0, 3, 1, 2))

    def _gn(v, G=32, eps=1e-05):
        B_, C_, H_, W_ = v.shape
        g = v.reshape(B_, G, C_ // G, H_, W_)
        m = jnp.mean(g, axis=(2, 3, 4), keepdims=True)
        s = jnp.var(g, axis=(2, 3, 4), keepdims=True)
        return ((g - m) / jnp.sqrt(s + eps)).reshape(v.shape)

    def _ln_c(v, eps=1e-06):
        m = jnp.mean(v, axis=1, keepdims=True)
        s = jnp.var(v, axis=1, keepdims=True)
        return (v - m) / jnp.sqrt(s + eps)

    def _ln_t(v, eps=1e-05):
        m = jnp.mean(v, axis=-1, keepdims=True)
        s = jnp.var(v, axis=-1, keepdims=True)
        return (v - m) / jnp.sqrt(s + eps)

    def _to_tokens(v):
        B_, C_, H_, W_ = v.shape
        return v.reshape(B_, C_, H_ * W_).transpose(0, 2, 1)

    def _from_tokens(t, like):
        B_, C_, H_, W_ = like.shape
        return t.transpose(0, 2, 1).reshape(B_, C_, H_, W_)
    x = x + _L0_conv_ref(_gn(x), L0_conv_Wq, L0_conv_bq, L0_conv_Wk, L0_conv_bk, L0_conv_Wv, L0_conv_bv, L0_conv_Wp, L0_conv_bp)
    x = x + _L1_conv_ref(_gn(x), L1_conv_conv_w, L1_conv_conv_b, L1_conv_ln_g, L1_conv_ln_b, L1_conv_w1, L1_conv_b1, L1_conv_w2, L1_conv_b2)
    return x

_drawn_inputs = setup_inputs


def setup_inputs(seed=0):
    import zlib

    import numpy as np

    out = dict(_drawn_inputs(seed))
    spreads = {'L1_conv_ln_g': (1.0, 0.2), 'L1_conv_ln_b': (0.0, 0.1)}
    factors = {'L0_conv_bq': 8.0,
     'L0_conv_bk': 8.0,
     'L1_conv_conv_b': 3.369,
     'L1_conv_b1': 8.0,
     'L1_conv_b2': 6.578}
    for name, (base, spread) in spreads.items():
        noise = np.random.default_rng([zlib.crc32(name.encode()), seed]).standard_normal(out[name].shape)
        drawn = base * np.exp(spread * noise) if base else spread * noise
        out[name] = jnp.asarray(drawn.astype(out[name].dtype))
    for name, factor in factors.items():
        out[name] = (out[name] * factor).astype(out[name].dtype)
    return out
```

```python
from contextlib import ExitStack

import concourse.bass as bass
from concourse import mybir

F32 = mybir.dt.float32
BF16 = mybir.dt.bfloat16
ACT = mybir.ActivationFunctionType
ALU = mybir.AluOpType
AX = mybir.AxisListType

P = 128
B = 2
HEADS, D = 8, 16
SIDE = 32
N = SIDE * SIDE
T = B * HEADS
NT = N // P
HALF = N // 2
PARTS = 3
STACK = 6 * D
ROWS = STACK + PARTS
Q_ORDER = (0, 1, 2, 0, 1, 0)
K_ORDER = (0, 0, 0, 1, 1, 2)
SCALE = float(D) ** -0.5
VW = 32
PR = 4
KS = 7
PAD = KS // 2
WIDE = SIDE + 2 * PAD
PADDED = WIDE * WIDE
SHIFTS = 4
CG = P // SHIFTS
GROUPS = P // CG
SPAN = 2
TAPS = GROUPS * KS * SPAN
HID = 4 * P
FC = HID // P
GN_EPS = 1e-5
LN_EPS = 1e-6

(C_WQ, C_WK, C_WV, C_WP, C_ID, C_CENTRE, C_GROUP, C_MEAN, C_ONES, C_MASK) = range(0, 10 * P, P)
C_TAPS = C_MASK + CG
C_COLS = C_TAPS + TAPS
(V_BQ, V_BK, V_BP, V_CB, V_G, V_B, V_B2, V_B1) = range(C_COLS, C_COLS + 8)
C_END = V_B1 + FC
MIDDLE = T // 4 + 1
OT_AT = 128


def build(nc, x, wpack, bvrow, ones3, w1, w2, out):
    parts_dram = nc.dram_tensor("parts_dram", (2, B, PARTS, HEADS, D, N), BF16, kind="Internal").ap()

    with ExitStack() as ctx:
        def sb(name, shape, dt=F32):
            return ctx.enter_context(nc.sbuf_tensor(name, shape, dt))

        def sem(name):
            return ctx.enter_context(nc.semaphore(name))

        xs = sb("xs", [P, B, N])
        xn = sb("xn", [P, B, N])
        w = sb("w", [P, C_END])
        bv = sb("bv", [1, P])
        rest = sb("rest", [P, 2, N])
        part = sb("part", [P, 2, PARTS, N], BF16)
        qs = sb("qs", [P, T * N], BF16)
        ks = sb("ks", [P, T * N], BF16)
        va = sb("va", [P, T * NT * VW])
        vh = sb("vh", [P, 2, NT, VW])
        pr = sb("pr", [P, PR, N])
        mx = sb("mx", [P, 2, NT])
        mres = sb("mres", [P, 2, NT])
        mlast = sb("mlast", [P, 2, NT])
        mparts = sb("mparts", [P, 2, PARTS * NT], BF16)
        mrows = sb("mrows", [PARTS * NT, 2, P], BF16)
        idb = sb("idb", [P, P], BF16)
        u = sb("u", [P, 2, 2 * P])
        rden = sb("rden", [P, 2, 4, 2])
        ot = sb("ot", [P, NT, T * D])
        oc = sb("oc", [P, B, N])
        x1 = xs
        xpad = sb("xpad", [P, PADDED + SHIFTS])
        xr = sb("xr", [P, GROUPS, PADDED + SHIFTS])
        wt = sb("wt", [P, TAPS, CG])
        gn_tiles = {k: [sb(f"{k}_{n}", [P, m]) for n, m in (("stats", 12), ("chan", 2), ("dev", 1), ("spread", 1), ("vareps", 1), ("rstd", 1))]
                    for k in ("in0", "in1", "mid0", "mid1")}
        vareps = sb("vareps", [P, B, NT])
        rstd = sb("rstd", [P, B, NT])
        zeros = sb("zeros", [P, NT])
        power = sb("power", [P, NT])
        b1s = sb("b1s", [P, FC])
        w1s = sb("w1s", [P, HID])
        w1g = sb("w1g", [P, HID])
        w2s = sb("w2s", [P, FC, P])
        ps = ctx.enter_context(nc.psum_tensor("ps", [P, 8, HALF], F32))
        sm = [ps[:, 2 * i:2 * i + 2, :].rearrange("p a n -> p (a n)") for i in range(2)]
        st = [ps[:, 4 + i, :] for i in range(2)]
        pv = ps[:, 6, :]
        mi = ps[:, 7, :]

        mt = mi[0:PARTS * NT, 0:P // 2].bitcast(BF16)
        otp = mi[:, OT_AT:OT_AT + 2 * P].rearrange("p (k q v) -> p q k v", q=4, v=VW)
        y = [rest[:, b, :] for b in range(B)]
        whole = part[:, :, :, :].rearrange("p i n c -> p (i n c)").bitcast(F32)
        yc = [whole[:, b * N:(b + 1) * N] for b in range(B)]
        sq = y
        yn = xn
        diag = whole[:, B * N:(B + 1) * N]
        hid = pr
        fin = [oc[:, b, :] for b in range(B)]
        lower = ps[:, 4:6, :].rearrange("p a n -> p (a n)")
        conv_out = [sm[0], lower]
        scale_out = [sm[0], lower]
        mlp_out = lower

        ident = w[:, C_ID:C_ID + P]
        centre = w[:, C_CENTRE:C_CENTRE + P]
        group = w[:, C_GROUP:C_GROUP + P]
        ones = w[:, C_ONES:C_ONES + P]
        spreadm = ones

        def vec(c, n=1):
            return w[:, c:c + n]


        made = {}

        def S(name, b=None):
            full = name if b is None else f"{name}_{b}"
            if full not in made:
                made[full] = sem(full)
            return made[full]

        s_ready = sem("s_ready")
        max_done = sem("max_done")
        m_step = sem("m_step")
        mt_ready = sem("mt_ready")
        mt_done = sem("mt_done")
        s_mrow = [sem(f"s_mrow{r}") for r in range(2)]
        st_ready = sem("st_ready")
        exp_done = sem("exp_done")
        pv_done = sem("pv_done")
        vh_ready = sem("vh_ready")
        u_ready = sem("u_ready")
        ot_ready = sem("ot_ready")
        rd_ready = sem("rd_ready")
        ot_done = sem("ot_done")

        block = ctx.enter_context(nc.Block())

        def later(t, n):
            return not isinstance(t, int) or t >= n

        def gn_dve(v, k, col, source, arrived, dest, done):
            stats, chan, dev, spread, ve, rs = gn_tiles[k]
            v.wait_ge(*arrived)
            for c in range(2):
                nc.vector.bn_stats(stats[:, 6 * c:6 * c + 6],
                                   source[:, c * HALF:(c + 1) * HALF]).then_inc(S(k + "_stats"), 1)
            v.wait_ge(S(k + "_stats"), 2)
            nc.vector.bn_aggr(chan[:, :], stats[:, :]).then_inc(S(k + "_chan"), 1)
            v.wait_ge(S(k + "_mean"), 1)
            v.wait_ge(S(k + "_chan"), 1)
            nc.vector.tensor_tensor(dev[:, :], chan[:, 0:1], mi[:, col:col + 1], ALU.subtract).then_inc(S(k + "_dev"), 1)
            v.wait_ge(S(k + "_dev"), 1)
            nc.vector.scalar_tensor_tensor(out=spread[:, :], in0=dev[:, :], scalar=dev[:, 0:1], in1=chan[:, 1:2],
                                           op0=ALU.mult, op1=ALU.add).then_inc(S(k + "_spread"), 1)
            v.wait_ge(S(k + "_var"), 1)
            nc.vector.tensor_scalar(ve[:, :], mi[:, col + 1:col + 2], GN_EPS, None, ALU.add).then_inc(S(k + "_ve"), 1)
            v.wait_ge(S(k + "_rstd"), 1)
            if len(dest.shape) == 3:
                source = source.rearrange("p (a c) -> p a c", c=SIDE)
            nc.vector.tensor_scalar(dest, source, mi[:, col:col + 1], rs[:, 0:1],
                                    ALU.subtract, ALU.mult).then_inc(done, 1)

        def gn_pe(t, k, col):
            _, chan, _, spread, _, _ = gn_tiles[k]
            t.wait_ge(S(k + "_chan"), 1)
            nc.tensor.matmul(mi[:, col:col + 1], group, chan[:, 0:1], start=True, stop=True).then_inc(S(k + "_mean"), 1)
            t.wait_ge(S(k + "_spread"), 1)
            nc.tensor.matmul(mi[:, col + 1:col + 2], group, spread[:, :], start=True, stop=True)\
                .then_inc(S(k + "_var"), 1)

        def gn_pool(g, k):
            ve, rs = gn_tiles[k][4:]
            g.wait_ge(S(k + "_ve"), 1)
            nc.gpsimd.tensor_tensor(rs[:, :], ve[:, :], power[:, 0:1], ALU.pow).then_inc(S(k + "_rstd"), 1)

        @block.sync
        def _(sp):
            sp.dma_start(xs[:, 0, :], x[0]).then_inc(S("x", 0), 16)
            sp.dma_start(w[:, :], wpack).then_inc(S("w"), 16)
            sp.dma_start(xs[:, 1, :], x[1]).then_inc(S("x", 1), 16)
            sp.dma_start(bv[:, :], bvrow).then_inc(S("bv"), 16)
            sp.dma_start(ks[STACK:ROWS, :], ones3).then_inc(S("kones"), 16)
            for b in range(B):
                for i in range(2):
                    for n in range(PARTS):
                        sp.wait_ge(S(f"part{i}{n}", b), 1)
                        sp.dma_start(parts_dram[i, b, n].rearrange("h d n -> (h d) n"),
                                     part[:, i, n, :]).then_inc(S("parts", b), 16)
                sp.wait_ge(S("parts", b), 2 * PARTS * 16)
                for order, dst, i in ((Q_ORDER, qs, 0), (K_ORDER, ks, 1)):
                    for g, n in enumerate(order):
                        sp.dma_start(
                            dst[g * D:(g + 1) * D, b * HEADS * N:(b + 1) * HEADS * N]
                            .rearrange("d (h n) -> d h n", n=N),
                            parts_dram[i, b, n].rearrange("h d n -> d h n")).then_inc(S("stack", b), 16)
            sp.dma_start(w1s[:, :], w1).then_inc(S("w12"), 16)
            sp.dma_start(w2s[:, :, :], w2.rearrange("(f p) c -> p f c", p=P)).then_inc(S("w12"), 16)

            def row_max(s, r):
                sp.wait_ge(mt_done, s + 1)
                sp.dma_start(qs[STACK:ROWS, bass.ds(s * N, N)].rearrange("r (i p) -> r i p", p=P),
                             mrows[:, r, :]).then_inc(s_mrow[r], 16)

            row_max(0, 0)
            row_max(1, 1)
            with sp.Fori(1, T // 2) as pair:
                row_max(2 * pair, 0)
                row_max(2 * pair + 1, 1)

            for b in range(B):
                sp.wait_ge(S("xpad", b), 1)
                if b:
                    sp.wait_ge(S("conv", b - 1), 1)
                for g in range(GROUPS):
                    for s in range(SHIFTS):
                        sp.dma_start(xr[s * CG:(s + 1) * CG, g, 0:PADDED],
                                     xpad[g * CG:(g + 1) * CG, s:s + PADDED]).then_inc(S("rep", b), 16)
            for b in range(B):
                sp.wait_ge(S("fin", b), 1)
                sp.dma_start(out[b], fin[b]).then_inc(S("out"), 16)
            sp.wait_ge(S("out"), 16 * B)

        @block.gpsimd
        def _(g):
            nc.gpsimd.memset(power[:, :], -0.5).then_inc(S("power"), 1)
            nc.gpsimd.memset(zeros[:, :], 0.0).then_inc(S("power"), 1)
            nc.gpsimd.memset(va[:, :], 0.0).then_inc(S("va0"), 1)
            g.wait_ge(S("va0"), 1)
            nc.gpsimd.memset(va[:, :].rearrange("p (t v) -> p t v", v=VW)[:, :, D:D + 1], 1.0).then_inc(S("va0"), 1)
            g.wait_ge(S("power"), 2)
            g.wait_ge(S("w"), 16)
            nc.gpsimd.tensor_copy(idb[:, :], ident).then_inc(S("idb"), 1)
            for b in range(B):
                gn_pool(g, f"in{b}")
                for i in range(2):
                    g.wait_ge(S(f"rest{i}", b), 1)
                    nc.gpsimd.tensor_copy(part[:, i, 1, :], rest[:, i, :]).then_inc(S(f"part{i}1", b), 1)
            nc.gpsimd.memset(xpad[:, :], 0.0).then_inc(S("xpad0"), 1)
            nc.gpsimd.tensor_tensor(
                wt[:, :, :], w[:, C_TAPS:C_COLS].rearrange("p (m a) -> p m a", a=1).broadcast_to([P, TAPS, CG]),
                w[:, C_MASK:C_MASK + CG].rearrange("p (a c) -> p a c", a=1).broadcast_to([P, TAPS, CG]),
                ALU.mult).then_inc(S("wt"), 1)

            def split_max(s, r):
                if later(s, 2):
                    g.wait_ge(pv_done, NT * s - NT)
                    g.wait_ge(mt_ready, s - 1)
                g.wait_ge(max_done, NT * s + NT)
                hi, mid, lo = (mparts[:, r, n * NT:(n + 1) * NT] for n in range(PARTS))
                nc.gpsimd.tensor_tensor(hi, zeros[:, :], mx[:, r, :], ALU.subtract).then_inc(m_step, 1)
                g.wait_ge(m_step, 5 * s + 1)
                nc.gpsimd.tensor_tensor(mres[:, r, :], mx[:, r, :], hi, ALU.add).then_inc(m_step, 1)
                g.wait_ge(m_step, 5 * s + 2)
                nc.gpsimd.tensor_tensor(mid, zeros[:, :], mres[:, r, :], ALU.subtract).then_inc(m_step, 1)
                g.wait_ge(m_step, 5 * s + 3)
                nc.gpsimd.tensor_tensor(mlast[:, r, :], mres[:, r, :], mid, ALU.add).then_inc(m_step, 1)
                g.wait_ge(m_step, 5 * s + 4)
                nc.gpsimd.tensor_tensor(lo, zeros[:, :], mlast[:, r, :], ALU.subtract).then_inc(m_step, 1)

            def fetch_v(t, r):
                nc.gpsimd.tensor_copy(vh[:, r, :, :].rearrange("p j v -> p (j v)"),
                                      va[:, bass.ds(t * (NT * VW), NT * VW)]).then_inc(vh_ready, 1)

            split_max(0, 0)
            for b in range(B):
                g.wait_ge(S("va", b), 1)
            g.wait_ge(S("va0"), 2)
            fetch_v(0, 0)
            split_max(1, 1)
            fetch_v(1, 1)
            with g.Fori(1, T // 2) as pair:
                split_max(2 * pair, 0)
                fetch_v(2 * pair, 0)
                split_max(2 * pair + 1, 1)
                fetch_v(2 * pair + 1, 1)
            for b in range(B):
                gn_pool(g, f"mid{b}")
            for b in range(B):
                g.wait_ge(S("ln_ve", b), 1)
                nc.gpsimd.tensor_tensor(rstd[:, b, :], vareps[:, b, :], power[:, :], ALU.pow).then_inc(S("ln_rstd", b), 1)

        @block.scalar
        def _(a):
            a.wait_ge(S("w"), 16)
            a.wait_ge(S("va0"), 2)
            for b in range(B):
                for i in range(2):
                    a.wait_ge(S(f"proj{i}", b), 1)
                    if b:
                        a.wait_ge(S("parts", b - 1), 2 * PARTS * 16)
                    nc.scalar.activation(part[:, i, 0, :], sm[i], ACT.Identity, bias=vec(V_BQ + i)).then_inc(S(f"part{i}0", b), 1)
                a.wait_ge(S("projv", b), 1)
                for c in range(2):
                    for j in range(4):
                        last = nc.scalar.activation(
                            va[:, :].rearrange("p (t j v) -> p j t v", j=NT, v=VW)
                            [:, 4 * c + j, b * HEADS:(b + 1) * HEADS, 0:D],
                            st[c][:, j * P:(j + 1) * P].rearrange("p (h d) -> p h d", d=D), ACT.Copy)
                last.then_inc(S("va", b), 1)

            def copy_max(s, r):
                a.wait_ge(mt_ready, s + 1)
                if later(s, 2):
                    a.wait_ge(s_mrow[r], (s - r) * 8)
                nc.scalar.activation(mrows[:, r, :], mt, ACT.Copy).then_inc(mt_done, 1)

            def copy_u(t, r):
                a.wait_ge(pv_done, NT * t + NT)
                if later(t, 2):
                    a.wait_ge(ot_ready, t - 1)
                nc.scalar.activation(u[:, r, :], pv[:, 0:2 * P], ACT.Copy).then_inc(u_ready, 1)

            def head(t, r, last=False):
                for j in range(NT):
                    for c in range(2):
                        a.wait_ge(st_ready, 2 * NT * t + (2 * j + c + 1))
                        if c == 0 and not (isinstance(t, int) and NT * t + j < PR):
                            a.wait_ge(pv_done, NT * t + (j - PR + 1))
                        nc.scalar.activation(pr[:, j % PR, c * HALF:(c + 1) * HALF], st[c], ACT.Exp,
                                             scale=SCALE).then_inc(exp_done, 1)
                    if j == 0 and later(t, 1):
                        copy_u(t - 1, 1 - r)
                    if j == 4 and not last:
                        copy_max(t + 1, 1 - r)

            def finish(b):
                a.wait_ge(S("ot_T", b), 1)
                nc.scalar.activation(oc[:, b, :], sm[0], ACT.Copy).then_inc(S("oc", b), 1)

            copy_max(0, 0)
            head(0, 0)
            head(1, 1)
            with a.Fori(1, MIDDLE) as pair:
                head(2 * pair, 0)
                head(2 * pair + 1, 1)
            finish(0)
            with a.Fori(MIDDLE, T // 2 - 1) as pair:
                head(2 * pair, 0)
                head(2 * pair + 1, 1)
            head(T - 2, 0)
            head(T - 1, 1, last=True)
            copy_u(T - 1, 1)
            finish(1)
            for b in range(B):
                a.wait_ge(S("conv", b), 1)
                nc.scalar.activation(y[b], conv_out[b], ACT.Identity, bias=vec(V_CB)).then_inc(S("y", b), 1)
                a.wait_ge(S("centred", b), 1)
                nc.scalar.activation(sq[b], sm[1], ACT.Square).then_inc(S("sq", b), 1)
                nc.scalar.activation(yc[b], sm[1], ACT.Copy).then_inc(S("yc", b), 1)
            for b in range(B):
                for f in range(FC):
                    a.wait_ge(S(f"hid{f}", b), 1)
                    if b:
                        a.wait_ge(S("mlp", 0), 1)
                    a.wait_ge(S("b1"), 1)
                    nc.scalar.activation(hid[:, f, :], sm[f % 2], ACT.Gelu, bias=b1s[:, f:f + 1]).then_inc(S(f"gelu{f}", b), 1)

        @block.vector
        def _(v):
            def split(b):
                for i in range(2):
                    v.wait_ge(S(f"proj{i}", b), 1)
                    if b:
                        v.wait_ge(S(f"part{i}1", b - 1), 1)
                    v.wait_ge(S(f"part{i}0", b), 1)
                    nc.vector.scalar_tensor_tensor(out=rest[:, i, :], in0=sm[i], scalar=vec(V_BQ + i),
                                                   in1=part[:, i, 0, :], op0=ALU.add, op1=ALU.subtract)\
                        .then_inc(S(f"rest{i}", b), 1)
                for i in range(2):
                    v.wait_ge(S(f"part{i}1", b), 1)
                    v.wait_ge(S(f"rest{i}", b), 1)
                    nc.vector.tensor_tensor(part[:, i, 2, :], rest[:, i, :], part[:, i, 1, :], ALU.subtract)\
                        .then_inc(S(f"part{i}2", b), 1)

            v.wait_ge(S("w"), 16)
            for b in range(B):
                gn_dve(v, f"in{b}", 2 * b, xs[:, b, :], (S("x", b), 16), xn[:, b, :], S("xn", b))
                split(b)

            def maxima(s, r, i):
                v.wait_ge(s_ready, NT * s + (i + 1))
                if i == 0 and later(s, 2):
                    v.wait_ge(m_step, 5 * s - 5)
                nc.vector.tensor_reduce(mx[:, r, i:i + 1], sm[i % 2], AX.X, ALU.max).then_inc(max_done, 1)

            def normalise(t, r):
                v.wait_ge(ot_ready, t + 1)
                nc.vector.reciprocal(rden[:, r, :, :], otp[:, :, :, D]).then_inc(rd_ready, 1)
                v.wait_ge(rd_ready, t + 1)
                nc.vector.tensor_tensor(
                    ot[:, :, bass.ds(t * D, D)].rearrange("p (q k) d -> p q k d", k=2),
                    otp[:, :, :, 0:D],
                    rden[:, r, :, :].rearrange("p q (k a) -> p q k a", a=1).broadcast_to([P, 4, 2, D]), ALU.mult).then_inc(ot_done, 1)

            def head(t, r, ahead=True):
                for i in range(NT):
                    if ahead:
                        maxima(t + 2, r, i)
                    if i == 2 and later(t, 1):
                        normalise(t - 1, 1 - r)

            def finish(b):
                v.wait_ge(S("projp", b), 1)
                nc.vector.scalar_tensor_tensor(out=x1[:, b, :], in0=sm[1], scalar=vec(V_BP), in1=xs[:, b, :],
                                               op0=ALU.add, op1=ALU.add).then_inc(S("x1", b), 1)

            def norm_mid(b):
                if b:
                    v.wait_ge(S("rep", b - 1), 16 * GROUPS * SHIFTS)
                v.wait_ge(S("xpad0"), 1)
                inner = xpad[:, 0:PADDED].rearrange("p (a c) -> p a c", c=WIDE)[:, PAD:PAD + SIDE, PAD:PAD + SIDE]
                gn_dve(v, f"mid{b}", 4 + 2 * b, x1[:, b, :], (S("x1", b), 1), inner, S("xpad", b))

            for i in range(NT):
                maxima(0, 0, i)
            for i in range(NT):
                maxima(1, 1, i)
            head(0, 0)
            head(1, 1)
            with v.Fori(1, MIDDLE) as pair:
                head(2 * pair, 0)
                head(2 * pair + 1, 1)
            finish(0)
            with v.Fori(MIDDLE, T // 2 - 1) as pair:
                head(2 * pair, 0)
                head(2 * pair + 1, 1)
            head(T - 2, 0, ahead=False)
            head(T - 1, 1, ahead=False)
            normalise(T - 1, 1)
            norm_mid(0)
            v.wait_ge(S("w12"), 32)
            nc.vector.tensor_scalar(w1g[:, :], w1s[:, :], vec(V_G), None, ALU.mult).then_inc(S("w1g"), 1)
            v.wait_ge(S("lnb"), 1)
            nc.vector.tensor_tensor(b1s[:, :], pv[:, 0:FC], vec(V_B1, FC), ALU.add).then_inc(S("b1"), 1)
            finish(1)
            norm_mid(1)
            for b in range(B):
                v.wait_ge(S("ln_var", b), 1)
                nc.vector.tensor_scalar(vareps[:, b, :], pv[:, 32 + NT * b:32 + NT * b + NT], LN_EPS, None, ALU.add)\
                    .then_inc(S("ln_ve", b), 1)
                v.wait_ge(S("ln_rstd", b), 1)
                if b:
                    v.wait_ge(S("scale", b - 1), 1)
                nc.vector.tensor_tensor(
                    diag.rearrange("p (i c) -> p i c", c=P),
                    ident.rearrange("p (a c) -> p a c", a=1).broadcast_to([P, NT, P]),
                    rstd[:, b, :].rearrange("p (i a) -> p i a", a=1).broadcast_to([P, NT, P]), ALU.mult).then_inc(S("diag", b), 1)
                v.wait_ge(S("scale", b), 1)
                v.wait_ge(S("yc", b), 1)
                nc.vector.tensor_tensor(yn[:, b, :], yc[b], scale_out[b], ALU.mult).then_inc(S("yn", b), 1)
            for b in range(B):
                v.wait_ge(S("mlp", b), 1)
                nc.vector.scalar_tensor_tensor(out=fin[b], in0=mlp_out, scalar=vec(V_B2), in1=x1[:, b, :],
                                               op0=ALU.add, op1=ALU.add).then_inc(S("fin", b), 1)

        @block.tensor
        def _(t_):
            def project(b):
                t_.wait_ge(S("xn", b), 1)
                if b:
                    for i in range(2):
                        t_.wait_ge(S(f"part{i}0", b - 1), 1)
                        t_.wait_ge(S(f"rest{i}", b - 1), 1)
                    t_.wait_ge(S("va", b - 1), 1)
                for i in range(2):
                    for c in range(2):
                        last = nc.tensor.matmul(sm[i][:, c * HALF:(c + 1) * HALF], vec(C_WQ + i * P, P),
                                                xn[:, b, c * HALF:(c + 1) * HALF], start=True, stop=True)
                    last.then_inc(S(f"proj{i}", b), 1)
                t_.wait_ge(S("bv"), 16)
                for j in range(NT):
                    o = st[j // 4][:, (j % 4) * P:(j % 4 + 1) * P]
                    nc.tensor.matmul(o, xn[:, b, j * P:(j + 1) * P], vec(C_WV, P), start=True, stop=False)
                    last = nc.tensor.matmul(o, ones[0:1, :], bv[:, :], start=False, stop=True)
                last.then_inc(S("projv", b), 1)

            t_.wait_ge(S("w"), 16)
            for b in range(B):
                gn_pe(t_, f"in{b}", 2 * b)
                project(b)

            def scores(s, i):
                if not (isinstance(s, int) and NT * s + i < 2):
                    t_.wait_ge(max_done, NT * s + (i - 1))
                for c in range(2):
                    last = nc.tensor.matmul(sm[i % 2][:, c * HALF:(c + 1) * HALF],
                                            qs[0:STACK, bass.ds(s * N + i * P, P)],
                                            ks[0:STACK, bass.ds(s * N + c * HALF, HALF)], start=True, stop=True)
                last.then_inc(s_ready, 1)

            def turn_max(s, r):
                t_.wait_ge(m_step, 5 * s + 5)
                if later(s, 1):
                    t_.wait_ge(mt_done, s)
                if later(s, 2):
                    t_.wait_ge(ot_done, s - 1)
                nc.tensor.transpose(mt, mparts[:, r, :], idb[:, :]).then_inc(mt_ready, 1)

            def turn_u(t, r):
                t_.wait_ge(u_ready, t + 1)
                t_.wait_ge(mt_done, T if isinstance(t, int) and t == T - 1 else t + 2)
                if later(t, 1):
                    t_.wait_ge(ot_done, t)
                for i in range(2):
                    last = nc.tensor.transpose(mi[:, OT_AT + i * P:OT_AT + (i + 1) * P],
                                               u[:, r, i * P:(i + 1) * P], ident)
                last.then_inc(ot_ready, 1)

            def scores_t(t, j):
                for c in range(2):
                    if not (isinstance(t, int) and 2 * NT * t + 2 * j + c < 2):
                        t_.wait_ge(exp_done, 2 * NT * t + (2 * j + c - 1))
                    nc.tensor.matmul(st[c], ks[0:ROWS, bass.ds(t * N + j * P, P)],
                                     qs[0:ROWS, bass.ds(t * N + c * HALF, HALF)],
                                     start=True, stop=True).then_inc(st_ready, 1)

            def times_v(t, r, j):
                if j == 0:
                    t_.wait_ge(vh_ready, t + 1)
                    if later(t, 1):
                        t_.wait_ge(u_ready, t)
                t_.wait_ge(exp_done, 2 * NT * t + (2 * j + 2))
                for q in range(4):
                    last = nc.tensor.matmul(pv[q * VW:(q + 1) * VW, 0:2 * P], vh[:, r, j, :],
                                            pr[:, j % PR, 2 * P * q:2 * P * (q + 1)],
                                            start=(j == 0), stop=(j == NT - 1))
                last.then_inc(pv_done, 1)

            def head(t, r, ahead=True, last=False):
                for j in range(NT):
                    if j == 0:
                        t_.wait_ge(s_mrow[r], (t - r) * 8 + 16)
                    scores_t(t, j)
                    if j:
                        times_v(t, r, j - 1)
                    if j == 1 and later(t, 1):
                        turn_u(t - 1, 1 - r)
                    if j == 3 and not last:
                        turn_max(t + 1, 1 - r)
                    if ahead:
                        scores(t + 2, j)
                times_v(t, r, NT - 1)

            def finish(b):
                t_.wait_ge(ot_done, HEADS * (b + 1))
                t_.wait_ge(max_done, NT * T if b else NT * (2 * MIDDLE + 2))
                for i in range(NT):
                    last = nc.tensor.transpose(
                        sm[0][:, i * P:(i + 1) * P],
                        ot[:, i, b * P:(b + 1) * P], ident)
                last.then_inc(S("ot_T", b), 1)
                t_.wait_ge(S("oc", b), 1)
                for c in range(2):
                    last = nc.tensor.matmul(sm[1][:, c * HALF:(c + 1) * HALF], vec(C_WP, P),
                                            oc[:, b, c * HALF:(c + 1) * HALF], start=True, stop=True)
                last.then_inc(S("projp", b), 1)

            for i in range(2):
                t_.wait_ge(S(f"rest{i}", 1), 1)
                t_.wait_ge(S(f"part{i}0", 1), 1)
            t_.wait_ge(S("stack", 0), 16 * 12)
            t_.wait_ge(S("idb"), 1)
            for i in range(NT):
                scores(0, i)
            for i in range(NT):
                scores(1, i)
            turn_max(0, 0)
            t_.wait_ge(S("kones"), 16)
            t_.wait_ge(S("va", 1), 1)
            head(0, 0)
            head(1, 1)
            with t_.Fori(1, 3) as pair:
                head(2 * pair, 0)
                head(2 * pair + 1, 1)
            t_.wait_ge(S("stack", 1), 16 * 12)
            with t_.Fori(3, MIDDLE) as pair:
                head(2 * pair, 0)
                head(2 * pair + 1, 1)
            finish(0)
            t_.wait_ge(S("x1", 0), 1)
            with t_.Fori(MIDDLE, T // 2 - 1) as pair:
                head(2 * pair, 0)
                head(2 * pair + 1, 1)
            head(T - 2, 0, ahead=False)
            head(T - 1, 1, ahead=False, last=True)
            turn_u(T - 1, 1)

            def conv(b, half):
                for m in range(KS * SPAN):
                    dy, e = m // SPAN, m % SPAN
                    at = (dy + half * SIDE // 2) * WIDE + e * SHIFTS
                    for g in range(GROUPS):
                        rows = xr[:, g, at:at + SIDE // 2 * WIDE].rearrange("p (a c) -> p a c", c=WIDE)
                        last = nc.tensor.matmul(conv_out[b][g * CG:(g + 1) * CG, half * HALF:(half + 1) * HALF],
                                                wt[:, g * KS * SPAN + m, :], rows[:, :, 0:SIDE],
                                                start=(m == 0), stop=(m == KS * SPAN - 1))
                if half:
                    last.then_inc(S("conv", b), 1)

            def centre_out(b):
                t_.wait_ge(S("y", b), 1)
                if b:
                    t_.wait_ge(S("yc", b - 1), 1)
                for c in range(2):
                    last = nc.tensor.matmul(sm[1][:, c * HALF:(c + 1) * HALF], centre, y[b][:, c * HALF:(c + 1) * HALF],
                                            start=True, stop=True)
                last.then_inc(S("centred", b), 1)

            def ln_var(b):
                t_.wait_ge(S("sq", b), 1)
                t_.wait_ge(S("ln_ve", b - 1) if b else S("b1"), 1)
                for i in range(NT):
                    last = nc.tensor.matmul(pv[:, 32 + NT * b + i:32 + NT * b + i + 1], sq[b][:, i * P:(i + 1) * P],
                                            vec(C_MEAN), start=True, stop=True)
                last.then_inc(S("ln_var", b), 1)

            def ln_scale(b):
                t_.wait_ge(S("diag", b), 1)
                for c in range(2):
                    last = nc.tensor.matmul(scale_out[b][:, c * HALF:(c + 1) * HALF], spreadm,
                                            diag[:, c * HALF:(c + 1) * HALF], start=True, stop=True)
                last.then_inc(S("scale", b), 1)

            def mlp(b, f):
                if f == 0:
                    t_.wait_ge(S("yn", b), 1)
                    t_.wait_ge(S("w1g"), 1)
                if b or f >= 2:
                    t_.wait_ge(S(f"gelu{(f - 2) % FC}", b if f >= 2 else b - 1), 1)
                elif f == 1:
                    t_.wait_ge(S("yc", 1), 1)
                for c in range(2):
                    last = nc.tensor.matmul(sm[f % 2][:, c * HALF:(c + 1) * HALF], w1g[:, f * P:(f + 1) * P],
                                            yn[:, b, c * HALF:(c + 1) * HALF], start=True, stop=True)
                last.then_inc(S(f"hid{f}", b), 1)

            def mlp_down(b, f):
                t_.wait_ge(S(f"gelu{f}", b), 1)
                if f == 0:
                    t_.wait_ge(S("fin", 0) if b else S("yn", 1), 1)
                for c in range(2):
                    last = nc.tensor.matmul(mlp_out[:, c * HALF:(c + 1) * HALF], w2s[:, f, :],
                                            hid[:, f, c * HALF:(c + 1) * HALF], start=(f == 0), stop=(f == FC - 1),
                                            skip_group_check=True)
                if f == FC - 1:
                    last.then_inc(S("mlp", b), 1)

            gn_pe(t_, "mid0", 4)
            t_.wait_ge(S("w12"), 32)
            t_.wait_ge(u_ready, T)
            for f in range(FC):
                last = nc.tensor.matmul(pv[:, f:f + 1], w1s[:, f * P:(f + 1) * P], vec(V_B), start=True, stop=True)
            last.then_inc(S("lnb"), 1)
            finish(1)
            t_.wait_ge(S("wt"), 1)
            t_.wait_ge(S("rep", 0), 16 * GROUPS * SHIFTS)
            conv(0, 0)
            gn_pe(t_, "mid1", 6)
            conv(0, 1)
            centre_out(0)
            ln_var(0)
            t_.wait_ge(S("rep", 1), 16 * GROUPS * SHIFTS)
            conv(1, 0)
            ln_scale(0)
            conv(1, 1)
            centre_out(1)
            mlp(0, 0)
            ln_var(1)
            mlp(0, 1)
            mlp(0, 2)
            ln_scale(1)
            mlp(0, 3)
            for f in range(FC):
                mlp_down(0, f)
            mlp(1, 0)
            mlp(1, 1)
            for f in range(2, FC):
                mlp(1, f)
                mlp_down(1, f - 2)
            for f in range(2, FC):
                mlp_down(1, f)
    return nc


def kernel(**inputs):
    import numpy as np
    import concourse.bacc as bacc
    from concourse.bass_utils import run_bass_kernel_spmd

    def get(name):
        return np.ascontiguousarray(inputs[name])

    def heads_on_diagonal(m):
        full = np.zeros((P, P), m.dtype)
        for h in range(HEADS):
            full[h * D:(h + 1) * D, h * D:(h + 1) * D] = m[h].T
        return full

    f32 = np.float32
    eye = np.eye(P, dtype=f32)
    centre = (eye - np.full((P, P), 1.0 / P, f32)).astype(f32)
    in_group = np.kron(np.eye(P // 4, dtype=f32), np.full((4, 4), 0.25, f32))
    mask = np.tile(np.eye(CG, dtype=f32), (SHIFTS, 1))
    conv_w = get("L1_conv_conv_w").reshape(P, KS, KS)
    taps = np.zeros((SHIFTS, CG, GROUPS, KS, SPAN), conv_w.dtype)
    for s in range(SHIFTS):
        for e in range(SPAN):
            if e * SHIFTS + s < KS:
                taps[s, :, :, :, e] = conv_w[:, :, e * SHIFTS + s].reshape(GROUPS, CG, KS).transpose(1, 0, 2)
    columns = [get(n).reshape(P, 1) for n in ("L0_conv_bq", "L0_conv_bk", "L0_conv_bp", "L1_conv_conv_b",
                                              "L1_conv_ln_g", "L1_conv_ln_b", "L1_conv_b2")]
    wpack = np.concatenate(
        [heads_on_diagonal(get(f"L0_conv_W{n}")) for n in "qkvp"]
        + [eye, centre, in_group, np.full((P, P), 1.0 / P, f32), np.ones((P, P), f32), mask,
           taps.reshape(P, TAPS)]
        + columns + [get("L1_conv_b1").reshape(FC, P).T], axis=1)

    arrays = {
        "x": get("x").reshape(B, P, N),
        "wpack": np.ascontiguousarray(wpack),
        "bvrow": get("L0_conv_bv").reshape(1, P),
        "ones3": np.ones((PARTS, T * N), mybir.dt.np(BF16)),
        "w1": get("L1_conv_w1"),
        "w2": get("L1_conv_w2"),
    }
    nc = bacc.Bacc("TRN2", target_bir_lowering=False, num_devices=1)
    args = [nc.dram_tensor(n, a.shape, mybir.dt.from_np(a.dtype), kind="ExternalInput").ap()
            for n, a in arrays.items()]
    out = nc.dram_tensor("out", (B, P, N), F32, kind="ExternalOutput").ap()
    build(nc, *args, out)
    r = run_bass_kernel_spmd(nc, [arrays], core_ids=[0])
    return r.results[0]["out"].reshape(B, P, SIDE, SIDE)
```

```python
from contextlib import ExitStack

import concourse.bass as bass
from concourse import mybir

F32 = mybir.dt.float32
BF16 = mybir.dt.bfloat16
ACT = mybir.ActivationFunctionType
ALU = mybir.AluOpType
AX = mybir.AxisListType

P = 128
B = 2
HEADS, D = 8, 16
SIDE = 32
N = SIDE * SIDE
T = B * HEADS
NT = N // P
HALF = N // 2
PARTS = 3
STACK = 6 * D
ROWS = STACK + PARTS
Q_ORDER = (0, 1, 2, 0, 1, 0)
K_ORDER = (0, 0, 0, 1, 1, 2)
SCALE = float(D) ** -0.5
VW = 32
PR = 4
KS = 7
PAD = KS // 2
WIDE = SIDE + 2 * PAD
PADDED = WIDE * WIDE
SHIFTS = 4
CG = P // SHIFTS
GROUPS = P // CG
SPAN = 2
TAPS = GROUPS * KS * SPAN
HID = 4 * P
FC = HID // P
PE_ROWS = (4, 3)
DVE_ROWS = (2, 3)
POOL_ROWS = (1, 1)
GN_EPS = 1e-5
LN_EPS = 1e-6

(C_WQ, C_WK, C_WV, C_WP, C_ID, C_CENTRE, C_GROUP, C_MEAN, C_ONES, C_MASK) = range(0, 10 * P, P)
C_TAPS = C_MASK + CG
C_CONV = C_TAPS + TAPS
C_COLS = C_CONV + KS * KS
(V_BQ, V_BK, V_BP, V_CB, V_G, V_B, V_B2, V_B1) = range(C_COLS, C_COLS + 8)
C_END = V_B1 + FC
MIDDLE = T // 4 + 1
OT_AT = 128


def build(nc, x, wpack, bvrow, ones3, w1, w2, out):
    parts_dram = nc.dram_tensor("parts_dram", (2, B, PARTS, HEADS, D, N), BF16, kind="Internal").ap()

    with ExitStack() as ctx:
        def sb(name, shape, dt=F32):
            return ctx.enter_context(nc.sbuf_tensor(name, shape, dt))

        def sem(name):
            return ctx.enter_context(nc.semaphore(name))

        xs = sb("xs", [P, B, N])
        xn = sb("xn", [P, B, N])
        w = sb("w", [P, C_END])
        bv = sb("bv", [1, P])
        rest = sb("rest", [P, 2, N])
        part = sb("part", [P, 2, PARTS, N], BF16)
        qs = sb("qs", [P, T * N], BF16)
        ks = sb("ks", [P, T * N], BF16)
        va = sb("va", [P, T * NT * VW])
        vh = sb("vh", [P, 2, NT, VW])
        pr = sb("pr", [P, PR, N])
        mx = sb("mx", [P, 2, NT])
        mres = sb("mres", [P, 2, NT])
        mlast = sb("mlast", [P, 2, NT])
        mparts = sb("mparts", [P, 2, PARTS * NT], BF16)
        mrows = sb("mrows", [PARTS * NT, 2, P], BF16)
        idb = sb("idb", [P, P], BF16)
        u = sb("u", [P, 2, 2 * P])
        rden = sb("rden", [P, 2, 4, 2])
        ot = sb("ot", [P, NT, T * D])
        oc = sb("oc", [P, B, N])
        x1 = xs
        xpad = sb("xpad", [P, PADDED + SHIFTS])
        xr = sb("xr", [P, GROUPS, PADDED + SHIFTS])
        wt = sb("wt", [P, TAPS, CG])
        gn_tiles = [[sb(f"gn{k}_{n}", [P, m]) for n, m in (("stats", 12), ("chan", 2), ("dev", 1), ("spread", 1), ("vareps", 1), ("rstd", 1), ("mean", 1))]
                    for k in range(2 * B)]
        vareps = sb("vareps", [P, B, NT])
        rstd = sb("rstd", [P, B, NT])
        zeros = sb("zeros", [P, NT])
        power = sb("power", [P, NT])
        loaded = sb("loaded", [P, 1])
        warm = sb("warm", [P, HALF], BF16)
        b1s = sb("b1s", [P, FC])
        w1s = sb("w1s", [P, HID])
        w1g = sb("w1g", [P, HID])
        w2s = sb("w2s", [P, FC, P])
        ps = ctx.enter_context(nc.psum_tensor("ps", [P, 8, HALF], F32))
        sm = [ps[:, 2 * i:2 * i + 2, :].rearrange("p a n -> p (a n)") for i in range(2)]
        st = [ps[:, 4 + i, :] for i in range(2)]
        pv = ps[:, 6, :]
        mi = ps[:, 7, :]

        mt = mi[0:PARTS * NT, 0:P // 2].bitcast(BF16)
        otp = mi[:, OT_AT:OT_AT + 2 * P].rearrange("p (k q v) -> p q k v", q=4, v=VW)
        spare = qs[:, 0:HEADS * N].bitcast(F32)
        acc = [spare[:, b * N:(b + 1) * N] for b in range(B)]
        acc_pool = spare[:, 2 * N:3 * N]
        product = spare[:, 3 * N:4 * N]
        y = [rest[:, b, :] for b in range(B)]
        whole = part[:, :, :, :].rearrange("p i n c -> p (i n c)").bitcast(F32)
        yc = [whole[:, b * N:(b + 1) * N] for b in range(B)]
        sq = y
        yn = xn
        diag = whole[:, B * N:(B + 1) * N]
        hid = pr
        fin = [oc[:, b, :] for b in range(B)]
        lower = ps[:, 4:6, :].rearrange("p a n -> p (a n)")
        conv_out = [sm[0], lower]
        scale_out = [sm[0], lower]
        mlp_out = lower

        ident = w[:, C_ID:C_ID + P]
        centre = w[:, C_CENTRE:C_CENTRE + P]
        group = w[:, C_GROUP:C_GROUP + P]
        ones = w[:, C_ONES:C_ONES + P]
        spreadm = ones

        def vec(c, n=1):
            return w[:, c:c + n]

        def image(tile):
            return tile.rearrange("p (a c) -> p a c", c=SIDE)

        def window(dy, dx):
            return xpad[:, 0:PADDED].rearrange("p (a c) -> p a c", c=WIDE)[:, dy:dy + SIDE, dx:dx + SIDE]


        made = {}

        def S(name, b=None):
            full = name if b is None else f"{name}_{b}"
            if full not in made:
                made[full] = sem(full)
            return made[full]

        s_ready = sem("s_ready")
        max_done = sem("max_done")
        m_step = sem("m_step")
        mt_ready = sem("mt_ready")
        mt_done = sem("mt_done")
        s_mrow = [sem(f"s_mrow{r}") for r in range(2)]
        st_ready = sem("st_ready")
        exp_done = sem("exp_done")
        pv_done = sem("pv_done")
        vh_ready = sem("vh_ready")
        u_ready = sem("u_ready")
        ot_ready = sem("ot_ready")
        rd_ready = sem("rd_ready")
        ot_done = sem("ot_done")

        block = ctx.enter_context(nc.Block())

        def later(t, n):
            return not isinstance(t, int) or t >= n

        def gn_dve(v, n, source, arrived, dest, done):
            stats, chan, dev, spread, ve, rs, mean = gn_tiles[n]
            v.wait_ge(*arrived)
            for c in range(2):
                nc.vector.bn_stats(stats[:, 6 * c:6 * c + 6],
                                   source[:, c * HALF:(c + 1) * HALF]).then_inc(S("gn_stats"), 1)
            v.wait_ge(S("gn_stats"), 2 * n + 2)
            nc.vector.bn_aggr(chan[:, :], stats[:, :]).then_inc(S("gn_chan"), 1)
            v.wait_ge(S("gn_mean"), n + 1)
            v.wait_ge(S("gn_chan"), n + 1)
            nc.vector.tensor_copy(mean[:, :], mi[:, 2 * n:2 * n + 1]).then_inc(S("gn_mean2"), 1)
            v.wait_ge(S("gn_mean2"), n + 1)
            nc.vector.tensor_tensor(dev[:, :], chan[:, 0:1], mean[:, :], ALU.subtract).then_inc(S("gn_dev"), 1)
            v.wait_ge(S("gn_dev"), n + 1)
            nc.vector.scalar_tensor_tensor(out=spread[:, :], in0=dev[:, :], scalar=dev[:, 0:1], in1=chan[:, 1:2],
                                           op0=ALU.mult, op1=ALU.add).then_inc(S("gn_spread"), 1)
            v.wait_ge(S("gn_var"), n + 1)
            nc.vector.tensor_scalar(ve[:, :], mi[:, 2 * n + 1:2 * n + 2], GN_EPS, None, ALU.add).then_inc(S("gn_ve"), 1)
            v.wait_ge(S("gn_rstd"), n + 1)
            if len(dest.shape) == 3:
                source = source.rearrange("p (a c) -> p a c", c=SIDE)
            nc.vector.tensor_scalar(dest, source, mean[:, 0:1], rs[:, 0:1],
                                    ALU.subtract, ALU.mult).then_inc(done, 1)

        def gn_pe(t, n):
            _, chan, _, spread, _, _, _ = gn_tiles[n]
            t.wait_ge(S("gn_chan"), n + 1)
            nc.tensor.matmul(mi[:, 2 * n:2 * n + 1], group, chan[:, 0:1], start=True, stop=True).then_inc(S("gn_mean"), 1)
            t.wait_ge(S("gn_spread"), n + 1)
            nc.tensor.matmul(mi[:, 2 * n + 1:2 * n + 2], group, spread[:, :], start=True, stop=True)\
                .then_inc(S("gn_var"), 1)

        def gn_pool(g, n):
            ve, rs = gn_tiles[n][4:6]
            g.wait_ge(S("gn_ve"), n + 1)
            nc.gpsimd.tensor_tensor(rs[:, :], ve[:, :], power[:, 0:1], ALU.pow).then_inc(S("gn_rstd"), 1)

        @block.sync
        def _(sp):
            def send_parts(b):
                for n in range(PARTS):
                    for i in range(2):
                        sp.wait_ge(S(f"part{i}{n}", b), 1)
                        sp.dma_start(parts_dram[i, b, n].rearrange("h d n -> (h d) n"),
                                     part[:, i, n, :]).then_inc(S(f"sent{i}{n}", b), 16)

            def fetch_stack(b, lo, hi, done):
                for n in range(PARTS):
                    for i, (order, dst) in enumerate(((Q_ORDER, qs), (K_ORDER, ks))):
                        sp.wait_ge(S(f"sent{i}{n}", b), 16)
                        for g in range(STACK // D):
                            if order[g] == n:
                                sp.dma_start(
                                    dst[g * D:(g + 1) * D, (b * HEADS + lo) * N:(b * HEADS + hi) * N]
                                    .rearrange("d (h n) -> d h n", n=N),
                                    parts_dram[i, b, n, lo:hi].rearrange("h d n -> d h n")).then_inc(done, 16)

            sp.dma_start(xs[:, 0, :], x[0]).then_inc(S("x", 0), 16)
            sp.dma_start(w[:, :], wpack).then_inc(S("w"), 16)
            sp.dma_start(xs[:, 1, :], x[1]).then_inc(S("x", 1), 16)
            sp.dma_start(bv[:, :], bvrow).then_inc(S("bv"), 16)
            sp.dma_start(ks[STACK:ROWS, :], ones3).then_inc(S("kones"), 16)
            send_parts(0)
            fetch_stack(0, 0, 2, S("stack_first"))
            fetch_stack(0, 2, HEADS, S("stack", 0))
            sp.dma_start(w1s[:, :], w1).then_inc(S("w12"), 16)
            sp.dma_start(w2s[:, :, :], w2.rearrange("(f p) c -> p f c", p=P)).then_inc(S("w12"), 16)

            def row_max(s, r):
                sp.wait_ge(mt_done, s + 1)
                sp.dma_start(qs[STACK:ROWS, bass.ds(s * N, N)].rearrange("r (i p) -> r i p", p=P),
                             mrows[:, r, :]).then_inc(s_mrow[r], 16)

            row_max(0, 0)
            row_max(1, 1)
            send_parts(1)
            fetch_stack(1, 0, HEADS, S("stack", 1))
            with sp.Fori(1, T // 2) as pair:
                row_max(2 * pair, 0)
                row_max(2 * pair + 1, 1)

            for b in range(B):
                sp.wait_ge(S("xpad", b), 1)
                if b:
                    sp.wait_ge(S("conv", b - 1), 1)
                for g in range(GROUPS):
                    for s in range(SHIFTS):
                        sp.dma_start(xr[s * CG:(s + 1) * CG, g, 0:PADDED],
                                     xpad[g * CG:(g + 1) * CG, s:s + PADDED]).then_inc(S("rep", b), 16)
            for b in range(B):
                sp.wait_ge(S("fin", b), 1)
                sp.dma_start(out[b], fin[b]).then_inc(S("out"), 16)
            sp.wait_ge(S("out"), 16 * B)

        @block.gpsimd
        def _(g):
            nc.gpsimd.memset(power[:, :], -0.5).then_inc(S("power"), 1)
            nc.gpsimd.memset(zeros[:, :], 0.0).then_inc(S("power"), 1)
            nc.gpsimd.memset(warm[:, :], 0.0).then_inc(S("warm"), 1)
            nc.gpsimd.memset(va[:, :], 0.0).then_inc(S("va0"), 1)
            g.wait_ge(S("va0"), 1)
            nc.gpsimd.memset(va[:, :].rearrange("p (t v) -> p t v", v=VW)[:, :, D:D + 1], 1.0).then_inc(S("va0"), 1)
            g.wait_ge(S("power"), 2)
            g.wait_ge(S("w"), 16)
            nc.gpsimd.tensor_copy(idb[:, :], ident).then_inc(S("idb"), 1)
            for b in range(B):
                gn_pool(g, b)
            nc.gpsimd.memset(xpad[:, :], 0.0).then_inc(S("xpad0"), 1)
            nc.gpsimd.tensor_tensor(
                wt[:, :, :], w[:, C_TAPS:C_CONV].rearrange("p (m a) -> p m a", a=1).broadcast_to([P, TAPS, CG]),
                w[:, C_MASK:C_MASK + CG].rearrange("p (a c) -> p a c", a=1).broadcast_to([P, TAPS, CG]),
                ALU.mult).then_inc(S("wt"), 1)

            def split_max(s, r):
                if later(s, 2):
                    g.wait_ge(pv_done, NT * s - NT)
                    g.wait_ge(mt_ready, s - 1)
                g.wait_ge(max_done, NT * s + NT)
                hi, mid, lo = (mparts[:, r, n * NT:(n + 1) * NT] for n in range(PARTS))
                nc.gpsimd.tensor_tensor(hi, zeros[:, :], mx[:, r, :], ALU.subtract).then_inc(m_step, 1)
                g.wait_ge(m_step, 5 * s + 1)
                nc.gpsimd.tensor_tensor(mres[:, r, :], mx[:, r, :], hi, ALU.add).then_inc(m_step, 1)
                g.wait_ge(m_step, 5 * s + 2)
                nc.gpsimd.tensor_tensor(mid, zeros[:, :], mres[:, r, :], ALU.subtract).then_inc(m_step, 1)
                g.wait_ge(m_step, 5 * s + 3)
                nc.gpsimd.tensor_tensor(mlast[:, r, :], mres[:, r, :], mid, ALU.add).then_inc(m_step, 1)
                g.wait_ge(m_step, 5 * s + 4)
                nc.gpsimd.tensor_tensor(lo, zeros[:, :], mlast[:, r, :], ALU.subtract).then_inc(m_step, 1)

            def fetch_v(t, r):
                nc.gpsimd.tensor_copy(vh[:, r, :, :].rearrange("p j v -> p (j v)"),
                                      va[:, bass.ds(t * (NT * VW), NT * VW)]).then_inc(vh_ready, 1)

            split_max(0, 0)
            for b in range(B):
                g.wait_ge(S("va", b), 1)
            g.wait_ge(S("va0"), 2)
            fetch_v(0, 0)
            split_max(1, 1)
            fetch_v(1, 1)
            made_taps = []

            def conv_taps(b, n):
                first = KS - POOL_ROWS[b]
                for k in range(len(made_taps), min(len(made_taps) + n, POOL_ROWS[b] * KS)):
                    dy, dx = first + k // KS, k % KS
                    weight = w[:, C_CONV + dy * KS + dx:C_CONV + dy * KS + dx + 1]
                    if k == 0:
                        g.wait_ge(S("xpad", b), 1)
                        if b:
                            g.wait_ge(S("acc", b - 1), 1)
                        nc.gpsimd.tensor_scalar(image(acc_pool), window(dy, dx), weight, 0.0, ALU.mult, ALU.add)\
                            .then_inc(S("pool_tap", b), 1)
                    else:
                        g.wait_ge(S("pool_tap", b), k)
                        nc.gpsimd.tensor_scalar(image(product), window(dy, dx), weight, 0.0, ALU.mult, ALU.add)\
                            .then_inc(S("pool_product", b), 1)
                        g.wait_ge(S("pool_product", b), k)
                        nc.gpsimd.tensor_tensor(acc_pool, acc_pool, product, ALU.add).then_inc(S("pool_tap", b), 1)
                    made_taps.append(k)

            with g.Fori(1, MIDDLE + 2) as pair:
                split_max(2 * pair, 0)
                fetch_v(2 * pair, 0)
                split_max(2 * pair + 1, 1)
                fetch_v(2 * pair + 1, 1)
            gn_pool(g, B)
            for s in (T - 2, T - 1):
                split_max(s, s % 2)
                fetch_v(s, s % 2)
                conv_taps(0, 2)
            conv_taps(0, KS * KS)
            gn_pool(g, B + 1)
            made_taps.clear()
            conv_taps(1, KS * KS)
            for b in range(B):
                g.wait_ge(S("ln_ve", b), 1)
                nc.gpsimd.tensor_tensor(rstd[:, b, :], vareps[:, b, :], power[:, :], ALU.pow).then_inc(S("ln_rstd", b), 1)

        @block.scalar
        def _(a):
            a.wait_ge(S("power"), 2)
            nc.scalar.activation(loaded[:, :], zeros[:, 0:1], ACT.Exp).then_inc(S("loaded"), 1)
            a.wait_ge(S("w"), 16)
            a.wait_ge(S("va0"), 2)
            for b in range(B):
                for i in range(2):
                    a.wait_ge(S(f"proj{i}", b), 1)
                    if b:
                        a.wait_ge(S(f"sent{i}0", b - 1), 16)
                    nc.scalar.activation(part[:, i, 0, :], sm[i], ACT.Identity, bias=vec(V_BQ + i)).then_inc(S(f"part{i}0", b), 1)
                a.wait_ge(S("projv", b), 1)
                for c in range(2):
                    for j in range(4):
                        last = nc.scalar.activation(
                            va[:, :].rearrange("p (t j v) -> p j t v", j=NT, v=VW)
                            [:, 4 * c + j, b * HEADS:(b + 1) * HEADS, 0:D],
                            st[c][:, j * P:(j + 1) * P].rearrange("p (h d) -> p h d", d=D), ACT.Copy)
                last.then_inc(S("va", b), 1)

            def copy_max(s, r):
                a.wait_ge(mt_ready, s + 1)
                if later(s, 2):
                    a.wait_ge(s_mrow[r], (s - r) * 8)
                nc.scalar.activation(mrows[:, r, :], mt, ACT.Copy).then_inc(mt_done, 1)

            def copy_u(t, r):
                a.wait_ge(pv_done, NT * t + NT)
                if later(t, 2):
                    a.wait_ge(ot_ready, t - 1)
                nc.scalar.activation(u[:, r, :], pv[:, 0:2 * P], ACT.Copy).then_inc(u_ready, 1)

            def head(t, r, last=False):
                for j in range(NT):
                    for c in range(2):
                        a.wait_ge(st_ready, 2 * NT * t + (2 * j + c + 1))
                        if c == 0 and not (isinstance(t, int) and NT * t + j < PR):
                            a.wait_ge(pv_done, NT * t + (j - PR + 1))
                        nc.scalar.activation(pr[:, j % PR, c * HALF:(c + 1) * HALF], st[c], ACT.Exp,
                                             scale=SCALE).then_inc(exp_done, 1)
                    if j == 0 and later(t, 1):
                        copy_u(t - 1, 1 - r)
                    if j == 3 and not last:
                        copy_max(t + 1, 1 - r)

            def finish(b):
                a.wait_ge(S("ot_T", b), 1)
                nc.scalar.activation(oc[:, b, :], sm[0], ACT.Copy).then_inc(S("oc", b), 1)

            copy_max(0, 0)
            head(0, 0)
            head(1, 1)
            with a.Fori(1, MIDDLE) as pair:
                head(2 * pair, 0)
                head(2 * pair + 1, 1)
            finish(0)
            for t in range(2 * MIDDLE, T - 2):
                head(t, t % 2)
            head(T - 2, 0)
            head(T - 1, 1, last=True)
            copy_u(T - 1, 1)
            finish(1)
            for b in range(B):
                a.wait_ge(S("centred", b), 1)
                nc.scalar.activation(sq[b], sm[1], ACT.Square).then_inc(S("sq", b), 1)
                nc.scalar.activation(yc[b], sm[1], ACT.Copy).then_inc(S("yc", b), 1)
            for b in range(B):
                for f in range(FC):
                    a.wait_ge(S("hid"), FC * b + f + 1)
                    if b:
                        a.wait_ge(S("mlp", 0), 1)
                    a.wait_ge(S("b1"), 1)
                    nc.scalar.activation(hid[:, f, :], sm[f % 2], ACT.Gelu, bias=b1s[:, f:f + 1]).then_inc(S("gelu"), 1)

        @block.vector
        def _(v):
            def split_rest(b):
                for i in range(2):
                    v.wait_ge(S(f"proj{i}", b), 1)
                    v.wait_ge(S(f"part{i}0", b), 1)
                    nc.vector.scalar_tensor_tensor(out=rest[:, i, :], in0=sm[i], scalar=vec(V_BQ + i),
                                                   in1=part[:, i, 0, :], op0=ALU.add, op1=ALU.subtract)\
                        .then_inc(S(f"rest{i}", b), 1)

            def split_parts(b):
                for i in range(2):
                    v.wait_ge(S(f"rest{i}", b), 1)
                    if b:
                        v.wait_ge(S(f"sent{i}1", b - 1), 16)
                    nc.vector.tensor_copy(part[:, i, 1, :], rest[:, i, :]).then_inc(S(f"part{i}1", b), 1)
                for i in range(2):
                    v.wait_ge(S(f"part{i}1", b), 1)
                    if b:
                        v.wait_ge(S(f"sent{i}2", b - 1), 16)
                    nc.vector.tensor_tensor(part[:, i, 2, :], rest[:, i, :], part[:, i, 1, :], ALU.subtract)\
                        .then_inc(S(f"part{i}2", b), 1)

            v.wait_ge(S("w"), 16)
            gn_dve(v, 0, xs[:, 0, :], (S("x", 0), 16), xn[:, 0, :], S("xn", 0))
            split_rest(0)
            split_parts(0)
            gn_dve(v, 1, xs[:, 1, :], (S("x", 1), 16), xn[:, 1, :], S("xn", 1))
            split_rest(1)

            def maxima(s, r, i):
                v.wait_ge(s_ready, NT * s + (i + 1))
                if i == 0 and later(s, 2):
                    v.wait_ge(m_step, 5 * s - 5)
                nc.vector.tensor_reduce(mx[:, r, i:i + 1], sm[i % 2], AX.X, ALU.max).then_inc(max_done, 1)

            def normalise(t, r):
                v.wait_ge(ot_ready, t + 1)
                nc.vector.reciprocal(rden[:, r, :, :], otp[:, :, :, D]).then_inc(rd_ready, 1)
                v.wait_ge(rd_ready, t + 1)
                nc.vector.tensor_tensor(
                    ot[:, :, bass.ds(t * D, D)].rearrange("p (q k) d -> p q k d", k=2),
                    otp[:, :, :, 0:D],
                    rden[:, r, :, :].rearrange("p q (k a) -> p q k a", a=1).broadcast_to([P, 4, 2, D]), ALU.mult).then_inc(ot_done, 1)

            def head(t, r, ahead=True):
                for i in range(NT):
                    if ahead:
                        maxima(t + 2, r, i)
                    if i == 5 and later(t, 1):
                        normalise(t - 1, 1 - r)

            def finish(b):
                v.wait_ge(S("projp", b), 1)
                nc.vector.scalar_tensor_tensor(out=x1[:, b, :], in0=sm[1], scalar=vec(V_BP), in1=xs[:, b, :],
                                               op0=ALU.add, op1=ALU.add).then_inc(S("x1", b), 1)

            def norm_mid(b):
                if b:
                    v.wait_ge(S("rep", b - 1), 16 * GROUPS * SHIFTS)
                    v.wait_ge(S("pool_tap", b - 1), POOL_ROWS[b - 1] * KS)
                v.wait_ge(S("xpad0"), 1)
                inner = xpad[:, 0:PADDED].rearrange("p (a c) -> p a c", c=WIDE)[:, PAD:PAD + SIDE, PAD:PAD + SIDE]
                gn_dve(v, B + b, x1[:, b, :], (S("x1", b), 1), inner, S("xpad", b))

            made_taps = []

            def conv_taps(b, n):
                for k in range(len(made_taps), min(len(made_taps) + n, DVE_ROWS[b] * KS)):
                    dy, dx = PE_ROWS[b] + k // KS, k % KS
                    weight = w[:, C_CONV + dy * KS + dx:C_CONV + dy * KS + dx + 1]
                    if k == 0:
                        v.wait_ge(S("xpad", b), 1)
                        if b == 0:
                            v.wait_ge(st_ready, 2 * NT * (HEADS + 1))
                        nc.vector.tensor_scalar(image(acc[b]), window(dy, dx), weight, vec(V_CB), ALU.mult, ALU.add)\
                            .then_inc(S("dve_tap", b), 1)
                    else:
                        v.wait_ge(S("dve_tap", b), k)
                        nc.vector.scalar_tensor_tensor(out=image(acc[b]), in0=window(dy, dx), scalar=weight,
                                                       in1=image(acc[b]), op0=ALU.mult, op1=ALU.add)\
                            .then_inc(S("dve_tap", b), 1)
                    made_taps.append(k)

            def conv_sum(b):
                v.wait_ge(S("dve_tap", b), DVE_ROWS[b] * KS)
                v.wait_ge(S("pool_tap", b), POOL_ROWS[b] * KS)
                nc.vector.tensor_tensor(acc[b], acc[b], acc_pool, ALU.add).then_inc(S("acc", b), 1)
                v.wait_ge(S("acc", b), 1)
                v.wait_ge(S("conv", b), 1)
                nc.vector.tensor_tensor(y[b], conv_out[b], acc[b], ALU.add).then_inc(S("y", b), 1)

            for i in range(NT):
                maxima(0, 0, i)
            for i in range(NT):
                maxima(1, 1, i)
            split_parts(1)
            head(0, 0)
            head(1, 1)
            with v.Fori(1, MIDDLE) as pair:
                head(2 * pair, 0)
                head(2 * pair + 1, 1)
            finish(0)
            for t in range(2 * MIDDLE, 2 * MIDDLE + 2):
                head(t, t % 2)
            norm_mid(0)
            for t in range(2 * MIDDLE + 2, T - 2):
                head(t, t % 2)
            conv_taps(0, KS)
            head(T - 2, 0, ahead=False)
            conv_taps(0, KS)
            head(T - 1, 1, ahead=False)
            conv_taps(0, KS * KS)
            normalise(T - 1, 1)
            v.wait_ge(S("w12"), 32)
            nc.vector.tensor_scalar(w1g[:, :], w1s[:, :], vec(V_G), None, ALU.mult).then_inc(S("w1g"), 1)
            v.wait_ge(S("lnb"), 1)
            nc.vector.tensor_tensor(b1s[:, :], pv[:, 0:FC], vec(V_B1, FC), ALU.add).then_inc(S("b1"), 1)

            def ln_root(b):
                v.wait_ge(S("ln_var", b), 1)
                nc.vector.tensor_scalar(vareps[:, b, :], pv[:, 32 + NT * b:32 + NT * b + NT], LN_EPS, None, ALU.add)\
                    .then_inc(S("ln_ve", b), 1)
                v.wait_ge(S("ln_ve", b), 1)
                v.wait_ge(S("ln_rstd", b), 1)
                if b:
                    v.wait_ge(S("scale", b - 1), 1)
                nc.vector.tensor_tensor(
                    diag.rearrange("p (i c) -> p i c", c=P),
                    ident.rearrange("p (a c) -> p a c", a=1).broadcast_to([P, NT, P]),
                    rstd[:, b, :].rearrange("p (i a) -> p i a", a=1).broadcast_to([P, NT, P]), ALU.mult)\
                    .then_inc(S("diag", b), 1)

            def ln_apply(b):
                v.wait_ge(S("scale", b), 1)
                v.wait_ge(S("yc", b), 1)
                nc.vector.tensor_tensor(yn[:, b, :], yc[b], scale_out[b], ALU.mult).then_inc(S("yn", b), 1)

            made_taps.clear()
            finish(1)
            norm_mid(1)
            conv_sum(0)
            conv_taps(1, 7)
            ln_root(0)
            conv_taps(1, 4)
            ln_apply(0)
            conv_taps(1, KS * KS)
            conv_sum(1)
            ln_root(1)
            ln_apply(1)
            for b in range(B):
                v.wait_ge(S("mlp", b), 1)
                nc.vector.scalar_tensor_tensor(out=fin[b], in0=mlp_out, scalar=vec(V_B2), in1=x1[:, b, :],
                                               op0=ALU.add, op1=ALU.add).then_inc(S("fin", b), 1)

        @block.tensor
        def _(t_):
            def project(b):
                t_.wait_ge(S("xn", b), 1)
                if b:
                    for i in range(2):
                        t_.wait_ge(S(f"part{i}0", b - 1), 1)
                        t_.wait_ge(S(f"rest{i}", b - 1), 1)
                    t_.wait_ge(S("va", b - 1), 1)
                for i in range(2):
                    for c in range(2):
                        last = nc.tensor.matmul(sm[i][:, c * HALF:(c + 1) * HALF], vec(C_WQ + i * P, P),
                                                xn[:, b, c * HALF:(c + 1) * HALF], start=True, stop=True)
                    last.then_inc(S(f"proj{i}", b), 1)
                t_.wait_ge(S("bv"), 16)
                for j in range(NT):
                    o = st[j // 4][:, (j % 4) * P:(j % 4 + 1) * P]
                    nc.tensor.matmul(o, xn[:, b, j * P:(j + 1) * P], vec(C_WV, P), start=True, stop=False)
                    last = nc.tensor.matmul(o, ones[0:1, :], bv[:, :], start=False, stop=True)
                last.then_inc(S("projv", b), 1)

            def keep_busy(n):
                for _ in range(n):
                    nc.tensor.matmul(pv, warm[:, 0:P], warm[:, :], start=True, stop=True)

            t_.wait_ge(S("warm"), 1)
            keep_busy(14)
            t_.wait_ge(S("w"), 16)
            for b in range(B):
                gn_pe(t_, b)
                if b == 0:
                    keep_busy(8)
                project(b)

            def scores(s, i):
                if not (isinstance(s, int) and NT * s + i < 2):
                    t_.wait_ge(max_done, NT * s + (i - 1))
                for c in range(2):
                    last = nc.tensor.matmul(sm[i % 2][:, c * HALF:(c + 1) * HALF],
                                            qs[0:STACK, bass.ds(s * N + i * P, P)],
                                            ks[0:STACK, bass.ds(s * N + c * HALF, HALF)], start=True, stop=True)
                last.then_inc(s_ready, 1)

            def turn_max(s, r):
                t_.wait_ge(m_step, 5 * s + 5)
                if later(s, 1):
                    t_.wait_ge(mt_done, s)
                if later(s, 3):
                    t_.wait_ge(ot_done, s - 2)
                nc.tensor.transpose(mt, mparts[:, r, :], idb[:, :]).then_inc(mt_ready, 1)

            def turn_u(t, r):
                t_.wait_ge(u_ready, t + 1)
                t_.wait_ge(mt_done, T if isinstance(t, int) and t >= T - 2 else t + 3)
                if later(t, 1):
                    t_.wait_ge(ot_done, t)
                for i in range(2):
                    last = nc.tensor.transpose(mi[:, OT_AT + i * P:OT_AT + (i + 1) * P],
                                               u[:, r, i * P:(i + 1) * P], ident)
                last.then_inc(ot_ready, 1)

            def scores_t(t, j):
                for c in range(2):
                    if not (isinstance(t, int) and 2 * NT * t + 2 * j + c < 2):
                        t_.wait_ge(exp_done, 2 * NT * t + (2 * j + c - 1))
                    nc.tensor.matmul(st[c], ks[0:ROWS, bass.ds(t * N + j * P, P)],
                                     qs[0:ROWS, bass.ds(t * N + c * HALF, HALF)],
                                     start=True, stop=True).then_inc(st_ready, 1)

            def times_v(t, r, j):
                if j == 0:
                    t_.wait_ge(vh_ready, t + 1)
                    if later(t, 1):
                        t_.wait_ge(u_ready, t)
                t_.wait_ge(exp_done, 2 * NT * t + (2 * j + 2))
                for q in range(4):
                    last = nc.tensor.matmul(pv[q * VW:(q + 1) * VW, 0:2 * P], vh[:, r, j, :],
                                            pr[:, j % PR, 2 * P * q:2 * P * (q + 1)],
                                            start=(j == 0), stop=(j == NT - 1))
                last.then_inc(pv_done, 1)

            def head(t, r, ahead=True, last=False):
                for j in range(NT):
                    if j == 0:
                        t_.wait_ge(s_mrow[r], (t - r) * 8 + 16)
                    scores_t(t, j)
                    if j:
                        times_v(t, r, j - 1)
                    if j == 2 and not last:
                        turn_max(t + 1, 1 - r)
                    if j == 5 and later(t, 1):
                        turn_u(t - 1, 1 - r)
                    if ahead:
                        scores(t + 2, j)
                times_v(t, r, NT - 1)

            def finish(b):
                t_.wait_ge(ot_done, HEADS * (b + 1))
                t_.wait_ge(max_done, NT * T if b else NT * (2 * MIDDLE + 2))
                for i in range(NT):
                    last = nc.tensor.transpose(
                        sm[0][:, i * P:(i + 1) * P],
                        ot[:, i, b * P:(b + 1) * P], ident)
                last.then_inc(S("ot_T", b), 1)
                t_.wait_ge(S("oc", b), 1)
                for c in range(2):
                    last = nc.tensor.matmul(sm[1][:, c * HALF:(c + 1) * HALF], vec(C_WP, P),
                                            oc[:, b, c * HALF:(c + 1) * HALF], start=True, stop=True)
                last.then_inc(S("projp", b), 1)

            for i in range(2):
                t_.wait_ge(S(f"rest{i}", 1), 1)
                t_.wait_ge(S(f"part{i}0", 1), 1)
            t_.wait_ge(S("stack_first"), 16 * 12)
            t_.wait_ge(S("idb"), 1)
            for i in range(NT):
                scores(0, i)
            for i in range(NT):
                scores(1, i)
            turn_max(0, 0)
            t_.wait_ge(S("kones"), 16)
            t_.wait_ge(S("stack", 0), 16 * 12)
            t_.wait_ge(S("va", 1), 1)
            head(0, 0)
            head(1, 1)
            with t_.Fori(1, 3) as pair:
                head(2 * pair, 0)
                head(2 * pair + 1, 1)
            t_.wait_ge(S("stack", 1), 16 * 12)
            with t_.Fori(3, MIDDLE) as pair:
                head(2 * pair, 0)
                head(2 * pair + 1, 1)
            finish(0)
            t_.wait_ge(S("x1", 0), 1)
            for t in range(2 * MIDDLE, 2 * MIDDLE + 2):
                head(t, t % 2)
            gn_pe(t_, B)
            t_.wait_ge(S("gn_ve"), B + 1)
            for t in range(2 * MIDDLE + 2, T - 2):
                head(t, t % 2)
            head(T - 2, 0, ahead=False)
            head(T - 1, 1, ahead=False, last=True)
            turn_u(T - 1, 1)

            def conv(b, half):
                for m in range(PE_ROWS[b] * SPAN):
                    dy, e = m // SPAN, m % SPAN
                    at = (dy + half * SIDE // 2) * WIDE + e * SHIFTS
                    for g in range(GROUPS):
                        rows = xr[:, g, at:at + SIDE // 2 * WIDE].rearrange("p (a c) -> p a c", c=WIDE)
                        last = nc.tensor.matmul(conv_out[b][g * CG:(g + 1) * CG, half * HALF:(half + 1) * HALF],
                                                wt[:, g * KS * SPAN + m, :], rows[:, :, 0:SIDE],
                                                start=(m == 0), stop=(m == PE_ROWS[b] * SPAN - 1))
                if half:
                    last.then_inc(S("conv", b), 1)

            def centre_out(b):
                t_.wait_ge(S("y", b), 1)
                if b:
                    t_.wait_ge(S("yc", b - 1), 1)
                for c in range(2):
                    last = nc.tensor.matmul(sm[1][:, c * HALF:(c + 1) * HALF], centre, y[b][:, c * HALF:(c + 1) * HALF],
                                            start=True, stop=True)
                last.then_inc(S("centred", b), 1)

            def ln_var(b):
                t_.wait_ge(S("sq", b), 1)
                t_.wait_ge(S("ln_ve", b - 1) if b else S("b1"), 1)
                for i in range(NT):
                    last = nc.tensor.matmul(pv[:, 32 + NT * b + i:32 + NT * b + i + 1], sq[b][:, i * P:(i + 1) * P],
                                            vec(C_MEAN), start=True, stop=True)
                last.then_inc(S("ln_var", b), 1)

            def ln_scale(b):
                t_.wait_ge(S("diag", b), 1)
                for c in range(2):
                    last = nc.tensor.matmul(scale_out[b][:, c * HALF:(c + 1) * HALF], spreadm,
                                            diag[:, c * HALF:(c + 1) * HALF], start=True, stop=True)
                last.then_inc(S("scale", b), 1)

            def mlp(b, f):
                if f == 0:
                    t_.wait_ge(S("yn", b), 1)
                    t_.wait_ge(S("w1g"), 1)
                if b or f >= 2:
                    t_.wait_ge(S("gelu"), FC * b + f - 1)
                elif f == 1:
                    t_.wait_ge(S("yc", 1), 1)
                for c in range(2):
                    last = nc.tensor.matmul(sm[f % 2][:, c * HALF:(c + 1) * HALF], w1g[:, f * P:(f + 1) * P],
                                            yn[:, b, c * HALF:(c + 1) * HALF], start=True, stop=True)
                last.then_inc(S("hid"), 1)

            def mlp_down(b, f):
                t_.wait_ge(S("gelu"), FC * b + f + 1)
                if f == 0:
                    t_.wait_ge(S("fin", 0) if b else S("yn", 1), 1)
                for c in range(2):
                    last = nc.tensor.matmul(mlp_out[:, c * HALF:(c + 1) * HALF], w2s[:, f, :],
                                            hid[:, f, c * HALF:(c + 1) * HALF], start=(f == 0), stop=(f == FC - 1),
                                            skip_group_check=True)
                if f == FC - 1:
                    last.then_inc(S("mlp", b), 1)

            t_.wait_ge(S("w12"), 32)
            t_.wait_ge(u_ready, T)
            for f in range(FC):
                last = nc.tensor.matmul(pv[:, f:f + 1], w1s[:, f * P:(f + 1) * P], vec(V_B), start=True, stop=True)
            last.then_inc(S("lnb"), 1)
            finish(1)
            t_.wait_ge(S("wt"), 1)
            t_.wait_ge(S("rep", 0), 16 * GROUPS * SHIFTS)
            conv(0, 0)
            gn_pe(t_, B + 1)
            conv(0, 1)
            centre_out(0)
            ln_var(0)
            t_.wait_ge(S("rep", 1), 16 * GROUPS * SHIFTS)
            conv(1, 0)
            ln_scale(0)
            conv(1, 1)
            centre_out(1)
            mlp(0, 0)
            ln_var(1)
            mlp(0, 1)
            mlp(0, 2)
            ln_scale(1)
            mlp(0, 3)
            for f in range(FC):
                mlp_down(0, f)
            mlp(1, 0)
            mlp(1, 1)
            for f in range(2, FC):
                mlp(1, f)
                mlp_down(1, f - 2)
            for f in range(2, FC):
                mlp_down(1, f)
    return nc


def kernel(**inputs):
    import numpy as np
    import concourse.bacc as bacc
    from concourse.bass_utils import run_bass_kernel_spmd

    def get(name):
        return np.ascontiguousarray(inputs[name])

    def heads_on_diagonal(m):
        full = np.zeros((P, P), m.dtype)
        for h in range(HEADS):
            full[h * D:(h + 1) * D, h * D:(h + 1) * D] = m[h].T
        return full

    f32 = np.float32
    eye = np.eye(P, dtype=f32)
    centre = (eye - np.full((P, P), 1.0 / P, f32)).astype(f32)
    in_group = np.kron(np.eye(P // 4, dtype=f32), np.full((4, 4), 0.25, f32))
    mask = np.tile(np.eye(CG, dtype=f32), (SHIFTS, 1))
    conv_w = get("L1_conv_conv_w").reshape(P, KS, KS)
    taps = np.zeros((SHIFTS, CG, GROUPS, KS, SPAN), conv_w.dtype)
    for s in range(SHIFTS):
        for e in range(SPAN):
            if e * SHIFTS + s < KS:
                taps[s, :, :, :, e] = conv_w[:, :, e * SHIFTS + s].reshape(GROUPS, CG, KS).transpose(1, 0, 2)
    columns = [get(n).reshape(P, 1) for n in ("L0_conv_bq", "L0_conv_bk", "L0_conv_bp", "L1_conv_conv_b",
                                              "L1_conv_ln_g", "L1_conv_ln_b", "L1_conv_b2")]
    wpack = np.concatenate(
        [heads_on_diagonal(get(f"L0_conv_W{n}")) for n in "qkvp"]
        + [eye, centre, in_group, np.full((P, P), 1.0 / P, f32), np.ones((P, P), f32), mask,
           taps.reshape(P, TAPS), conv_w.reshape(P, KS * KS)]
        + columns + [get("L1_conv_b1").reshape(FC, P).T], axis=1)

    arrays = {
        "x": get("x").reshape(B, P, N),
        "wpack": np.ascontiguousarray(wpack),
        "bvrow": get("L0_conv_bv").reshape(1, P),
        "ones3": np.ones((PARTS, T * N), mybir.dt.np(BF16)),
        "w1": get("L1_conv_w1"),
        "w2": get("L1_conv_w2"),
    }
    nc = bacc.Bacc("TRN2", target_bir_lowering=False, num_devices=1)
    args = [nc.dram_tensor(n, a.shape, mybir.dt.from_np(a.dtype), kind="ExternalInput").ap()
            for n, a in arrays.items()]
    out = nc.dram_tensor("out", (B, P, N), F32, kind="ExternalOutput").ap()
    build(nc, *args, out)
    r = run_bass_kernel_spmd(nc, [arrays], core_ids=[0])
    return r.results[0]["out"].reshape(B, P, SIDE, SIDE)
```

```python
from contextlib import ExitStack

import concourse.bass as bass
from concourse import mybir

F32 = mybir.dt.float32
BF16 = mybir.dt.bfloat16
ACT = mybir.ActivationFunctionType
ALU = mybir.AluOpType
AX = mybir.AxisListType

P = 128
B = 2
HEADS, D = 8, 16
SIDE = 32
N = SIDE * SIDE
T = B * HEADS
NT = N // P
HALF = N // 2
PARTS = 3
STACK = 6 * D
ROWS = STACK + PARTS
Q_ORDER = (0, 1, 2, 0, 1, 0)
K_ORDER = (0, 0, 0, 1, 1, 2)
SCALE = float(D) ** -0.5
VW = 32
PR = 4
KS = 7
PAD = KS // 2
WIDE = SIDE + 2 * PAD
PADDED = WIDE * WIDE
SHIFTS = 4
CG = P // SHIFTS
GROUPS = P // CG
SPAN = 2
TAPS = GROUPS * KS * SPAN
HID = 4 * P
FC = HID // P
PE_RUNS = (6, 8)
DVE_TAPS = (14, 12)
PE_TAPS = tuple(n // SPAN * KS + n % SPAN * SHIFTS for n in PE_RUNS)
PE_ROWS = tuple(-(-n // SPAN) for n in PE_RUNS)
ALONE = 8
POOL_TAPS = tuple(KS * KS - PE_TAPS[b] - DVE_TAPS[b] for b in range(B))
PIECES = ((0, 0, N), (1, 0, HALF), (1, HALF, N))
TOP = SIDE // 2 + PAD
GN_EPS = 1e-5
LN_EPS = 1e-6

(C_WQ, C_WK, C_WV, C_WP, C_ID, C_CENTRE, C_GROUP, C_MEAN, C_ONES, C_MASK) = range(0, 10 * P, P)
C_TAPS = C_MASK + CG
C_CONV = C_TAPS + TAPS
C_COLS = C_CONV + KS * KS
(V_BQ, V_BK, V_BP, V_CB, V_G, V_B, V_B2, V_B1) = range(C_COLS, C_COLS + 8)
C_END = V_B1 + FC
FINISH = HEADS + 1


OT_AT = 128
LAG = 3


def maxima_plan():
    tiles = [(s, i) for s in range(T) for i in range(NT)]
    first = [tiles.pop(0) for _ in range(2 * NT - LAG)]
    counts = [[1] * NT for _ in range(T)]
    counts[FINISH] = [1] * LAG + [0, 0, 1, 2, 1]
    for t in range(FINISH + 1, FINISH + 5):
        counts[t][NT - 1] = 2
    return first, [[[tiles.pop(0) for _ in range(n) if tiles] for n in head] for head in counts]


def turned(t):
    return LAG + 3 if t == FINISH + 1 else LAG + 2


def build(nc, x, wpack, bvrow, ones3, w1, w2, out):
    parts_dram = nc.dram_tensor("parts_dram", (2, B, PARTS, HEADS, D, N), BF16, kind="Internal").ap()
    pad_dram = nc.dram_tensor("pad_dram", (B, P, PADDED + SHIFTS), F32, kind="Internal").ap()

    first_tiles, plan = maxima_plan()

    with ExitStack() as ctx:
        def sb(name, shape, dt=F32):
            return ctx.enter_context(nc.sbuf_tensor(name, shape, dt))

        def sem(name):
            return ctx.enter_context(nc.semaphore(name))

        xs = sb("xs", [P, B, N])
        xn = sb("xn", [P, B, N])
        w = sb("w", [P, C_END])
        bv = sb("bv", [1, P])
        rest = sb("rest", [P, 2, N])
        part = sb("part", [P, 2, PARTS, N], BF16)
        qs = sb("qs", [P, T * N], BF16)
        ks = sb("ks", [P, T * N], BF16)
        va = sb("va", [P, T * NT * VW])
        pr = sb("pr", [P, PR, N])
        mx = sb("mx", [P, 2, NT])
        mres = sb("mres", [P, 2, NT])
        mlast = sb("mlast", [P, 2, NT])
        mparts = sb("mparts", [P, 2, PARTS * NT], BF16)
        mrows = sb("mrows", [PARTS * NT, 2, P], BF16)
        idb = sb("idb", [P, P], BF16)
        u = sb("u", [P, 2, 2 * P])
        rden = sb("rden", [P, 2, 4, 2])
        ot = sb("ot", [P, NT, T * D])
        oc = sb("oc", [P, B, N])
        x1 = xs
        xpad = sb("xpad", [P, PADDED + SHIFTS])
        xr = sb("xr", [P, GROUPS, PADDED + SHIFTS])
        wt = sb("wt", [P, TAPS, CG])
        gn_tiles = [[sb(f"gn{k}_{n}", [P, m]) for n, m in (("stats", 12), ("chan", 2), ("dev", 1), ("spread", 1), ("vareps", 1), ("rstd", 1), ("mean", 1))]
                    for k in range(2 * B)]
        variance = sb("variance", [P, len(PIECES), N // 4])
        vareps = sb("vareps", [P, len(PIECES), NT])
        rstd = sb("rstd", [P, len(PIECES), NT])
        zeros = sb("zeros", [P, NT])
        power = sb("power", [P, NT])
        loaded = sb("loaded", [P, 1])
        warm = sb("warm", [P, HALF], BF16)
        b1s = sb("b1s", [P, FC])
        w1s = sb("w1s", [P, HID])
        w1g = sb("w1g", [P, HID])
        w2s = sb("w2s", [P, FC, P])
        ps = ctx.enter_context(nc.psum_tensor("ps", [P, 8, HALF], F32))
        sm = [ps[:, 2 * i:2 * i + 2, :].rearrange("p a n -> p (a n)") for i in range(2)]
        st = [ps[:, 4 + i, :] for i in range(2)]
        pv = ps[:, 6, :]
        mi = ps[:, 7, :]

        mt = mi[0:PARTS * NT, 0:P // 2].bitcast(BF16)
        otp = mi[:, OT_AT:OT_AT + 2 * P].rearrange("p (k q v) -> p q k v", q=4, v=VW)
        spare = qs[:, 0:HEADS * N].bitcast(F32)
        acc = [spare[:, b * N:(b + 1) * N] for b in range(B)]
        acc_pool = spare[:, 2 * N:3 * N]
        product = spare[:, 3 * N:4 * N]
        products = [product, acc[1]]
        y = [rest[:, b, :] for b in range(B)]
        whole = part[:, :, :, :].rearrange("p i n c -> p (i n c)").bitcast(F32)
        yc = [whole[:, b * N:(b + 1) * N] for b in range(B)]
        sq = y
        yn = xn
        diag = whole[:, B * N:(B + 1) * N]
        hid = [ks[:, 0:HEADS * N].bitcast(F32).rearrange("p (f n) -> p f n", f=FC), pr]
        fin = [oc[:, b, :] for b in range(B)]
        lower = ps[:, 4:6, :].rearrange("p a n -> p (a n)")
        conv_out = sm[0]
        centred = sm[1]
        mlp_out = lower

        def var_out(k):
            return sm[0][:, 0:quarter(k)] if k == 0 else pv[:, P * k:P * k + quarter(k)]

        def scale_out(k):
            return sm[1] if k == 0 else mi

        def quarter(k):
            return (PIECES[k][2] - PIECES[k][1]) // 4

        def tiles(k):
            return (PIECES[k][2] - PIECES[k][1]) // P

        def var_turned(k):
            return sm[0][:, HALF:HALF + NT] if k == 0 else pv[:, 3 * P + NT * k:3 * P + NT * k + tiles(k)]

        ident = w[:, C_ID:C_ID + P]
        centre = w[:, C_CENTRE:C_CENTRE + P]
        group = w[:, C_GROUP:C_GROUP + P]
        ones = w[:, C_ONES:C_ONES + P]

        def vec(c, n=1):
            return w[:, c:c + n]

        def image(tile):
            return tile.rearrange("p (a c) -> p a c", c=SIDE)

        def window(k, tap):
            _, lo, hi = PIECES[k]
            dy, dx = tap // KS, tap % KS
            return xpad[:, 0:PADDED].rearrange("p (a c) -> p a c", c=WIDE)[
                :, lo // SIDE + dy:hi // SIDE + dy, dx:dx + SIDE]

        def weight(tap):
            return w[:, C_CONV + tap:C_CONV + tap + 1]


        made = {}

        def S(name, b=None):
            full = name if b is None else f"{name}_{b}"
            if full not in made:
                made[full] = sem(full)
            return made[full]

        s_ready = sem("s_ready")
        max_done = sem("max_done")
        m_step = sem("m_step")
        mt_ready = sem("mt_ready")
        mt_done = sem("mt_done")
        s_mrow = [sem(f"s_mrow{r}") for r in range(2)]
        st_ready = sem("st_ready")
        exp_done = sem("exp_done")
        pv_done = sem("pv_done")
        u_ready = sem("u_ready")
        ot_ready = sem("ot_ready")
        rd_ready = sem("rd_ready")
        ot_done = sem("ot_done")

        block = ctx.enter_context(nc.Block())

        def later(t, n):
            return not isinstance(t, int) or t >= n

        def gn_stats(v, n, source, arrived):
            stats, chan, _, _, _, _, _ = gn_tiles[n]
            for c in range(2):
                v.wait_ge(*arrived(c))
                nc.vector.bn_stats(stats[:, 6 * c:6 * c + 6],
                                   source[:, c * HALF:(c + 1) * HALF]).then_inc(S("gn_stats"), 1)
            v.wait_ge(S("gn_stats"), 2 * n + 2)
            nc.vector.bn_aggr(chan[:, :], stats[:, :]).then_inc(S("gn_chan"), 1)

        def gn_spread(v, n):
            _, chan, dev, spread, _, _, mean = gn_tiles[n]
            v.wait_ge(S("gn_mean"), n + 1)
            v.wait_ge(S("gn_chan"), n + 1)
            nc.vector.tensor_copy(mean[:, :], mi[:, 2 * n:2 * n + 1]).then_inc(S("gn_mean2"), 1)
            v.wait_ge(S("gn_mean2"), n + 1)
            nc.vector.tensor_tensor(dev[:, :], chan[:, 0:1], mean[:, :], ALU.subtract).then_inc(S("gn_dev"), 1)
            v.wait_ge(S("gn_dev"), n + 1)
            nc.vector.scalar_tensor_tensor(out=spread[:, :], in0=dev[:, :], scalar=dev[:, 0:1], in1=chan[:, 1:2],
                                           op0=ALU.mult, op1=ALU.add).then_inc(S("gn_spread"), 1)

        def gn_vareps(v, n):
            v.wait_ge(S("gn_var"), n + 1)
            nc.vector.tensor_scalar(gn_tiles[n][4][:, :], mi[:, 2 * n + 1:2 * n + 2], GN_EPS, None, ALU.add)\
                .then_inc(S("gn_ve"), 1)

        def gn_apply(v, n, source, dest, done):
            rs, mean = gn_tiles[n][5:7]
            v.wait_ge(S("gn_rstd"), n + 1)
            if len(dest.shape) == 2:
                nc.vector.tensor_scalar(dest, source, mean[:, 0:1], rs[:, 0:1],
                                        ALU.subtract, ALU.mult).then_inc(done, 1)
            else:
                for c in range(2):
                    rows = slice(c * SIDE // 2, (c + 1) * SIDE // 2)
                    nc.vector.tensor_scalar(dest[:, rows, :], image(source)[:, rows, :], mean[:, 0:1], rs[:, 0:1],
                                            ALU.subtract, ALU.mult).then_inc(done, 1)

        def gn_pe_mean(t, n):
            t.wait_ge(S("gn_chan"), n + 1)
            nc.tensor.matmul(mi[:, 2 * n:2 * n + 1], group, gn_tiles[n][1][:, 0:1], start=True, stop=True)\
                .then_inc(S("gn_mean"), 1)

        def gn_pe_var(t, n):
            t.wait_ge(S("gn_spread"), n + 1)
            nc.tensor.matmul(mi[:, 2 * n + 1:2 * n + 2], group, gn_tiles[n][3][:, :], start=True, stop=True)\
                .then_inc(S("gn_var"), 1)

        def gn_pool(g, n):
            ve, rs = gn_tiles[n][4:6]
            g.wait_ge(S("gn_ve"), n + 1)
            nc.gpsimd.tensor_tensor(rs[:, :], ve[:, :], power[:, 0:1], ALU.pow).then_inc(S("gn_rstd"), 1)

        @block.sync
        def _(sp):
            def send_parts(b, n):
                for i in range(2):
                    sp.wait_ge(S(f"part{i}{n}", b), 1)
                    sp.dma_start(parts_dram[i, b, n].rearrange("h d n -> (h d) n"),
                                 part[:, i, n, :]).then_inc(S(f"sent{i}{n}", b), 16)

            def fetch_stack(b, n, lo, hi, done):
                for i, (order, dst) in enumerate(((Q_ORDER, qs), (K_ORDER, ks))):
                    sp.wait_ge(S(f"sent{i}{n}", b), 16)
                    for g in range(STACK // D):
                        if order[g] == n:
                            sp.dma_start(
                                dst[g * D:(g + 1) * D, (b * HEADS + lo) * N:(b * HEADS + hi) * N]
                                .rearrange("d (h n) -> d h n", n=N),
                                parts_dram[i, b, n, lo:hi].rearrange("h d n -> d h n")).then_inc(done, 16)

            sp.dma_start(xs[:, 0, :], x[0]).then_inc(S("x", 0), 16)
            sp.dma_start(w[:, :], wpack).then_inc(S("w"), 16)
            sp.dma_start(xs[:, 1, :], x[1]).then_inc(S("x", 1), 16)
            sp.dma_start(bv[:, :], bvrow).then_inc(S("bv"), 16)
            sp.dma_start(ks[STACK:ROWS, :], ones3).then_inc(S("kones"), 16)
            send_parts(0, 0)
            send_parts(0, 1)
            fetch_stack(0, 0, 0, 2, S("stack_first"))
            send_parts(0, 2)
            fetch_stack(0, 1, 0, 2, S("stack_first"))
            fetch_stack(0, 2, 0, 2, S("stack_first"))
            for n in range(PARTS):
                fetch_stack(0, n, 2, HEADS, S("stack", 0))
            sp.dma_start(w1s[:, :], w1).then_inc(S("w12"), 16)
            sp.dma_start(w2s[:, :, :], w2.rearrange("(f p) c -> p f c", p=P)).then_inc(S("w12"), 16)

            def row_max(s, r):
                sp.wait_ge(mt_done, s + 1)
                sp.dma_start(qs[STACK:ROWS, bass.ds(s * N, N)].rearrange("r (i p) -> r i p", p=P),
                             mrows[:, r, :]).then_inc(s_mrow[r], 16)

            def replicate(b):
                ends = (0, TOP * WIDE, (SIDE + PE_ROWS[b] - 1) * WIDE)
                for h in range(2):
                    lo, hi = ends[h], ends[h + 1]
                    sp.wait_ge(S("xpad", b), h + 1)
                    sp.dma_start(pad_dram[b, :, lo + h * (SHIFTS - 1):hi + SHIFTS - 1],
                                 xpad[:, lo + h * (SHIFTS - 1):hi + SHIFTS - 1]).then_inc(S(f"pad_sent{h}", b), 16)
                for h in range(2):
                    lo, hi = ends[h], ends[h + 1]
                    sp.wait_ge(S(f"pad_sent{h}", b), 16)
                    if b:
                        sp.wait_ge(S("conv0", b - 1), 1)
                        sp.wait_ge(S("conv1", b - 1), 1)
                    for s in range(SHIFTS):
                        sp.dma_start(xr[s * CG:(s + 1) * CG, :, lo:hi],
                                     pad_dram[b, :, lo + s:hi + s].rearrange("(g c) n -> c g n", c=CG))\
                            .then_inc(S(f"rep{h}", b), 16)

            send_parts(1, 0)
            row_max(0, 0)
            send_parts(1, 1)
            for s in range(1, 4):
                row_max(s, s % 2)
            send_parts(1, 2)
            for n in range(PARTS):
                fetch_stack(1, n, 0, HEADS, S("stack", 1))
            with sp.Fori(2, T // 2 - 1) as pair:
                row_max(2 * pair, 0)
                row_max(2 * pair + 1, 1)

            replicate(0)
            for s in range(T - 2, T):
                row_max(s, s % 2)
            replicate(1)
            for k, (b, lo, hi) in enumerate(PIECES):
                sp.wait_ge(S("fin"), k + 1)
                sp.dma_start(out[b][:, lo:hi], fin[b][:, lo:hi]).then_inc(S("out"), 16)
            sp.wait_ge(S("out"), 16 * len(PIECES))

        @block.gpsimd
        def _(g):
            nc.gpsimd.memset(power[:, :], -0.5).then_inc(S("power"), 1)
            nc.gpsimd.memset(zeros[:, :], 0.0).then_inc(S("power"), 1)
            nc.gpsimd.memset(warm[:, :], 0.0).then_inc(S("warm"), 1)
            nc.gpsimd.memset(va[:, :], 0.0).then_inc(S("va0"), 1)
            g.wait_ge(S("va0"), 1)
            nc.gpsimd.memset(va[:, :].rearrange("p (t v) -> p t v", v=VW)[:, :, D:D + 1], 1.0).then_inc(S("va0"), 1)
            g.wait_ge(S("power"), 2)
            g.wait_ge(S("w"), 16)
            nc.gpsimd.tensor_copy(idb[:, :], ident).then_inc(S("idb"), 1)
            gn_pool(g, 0)
            gn_pool(g, 1)
            nc.gpsimd.memset(xpad[:, :], 0.0).then_inc(S("xpad0"), 1)
            nc.gpsimd.tensor_tensor(
                wt[:, :, :], w[:, C_TAPS:C_CONV].rearrange("p (m a) -> p m a", a=1).broadcast_to([P, TAPS, CG]),
                w[:, C_MASK:C_MASK + CG].rearrange("p (a c) -> p a c", a=1).broadcast_to([P, TAPS, CG]),
                ALU.mult).then_inc(S("wt"), 1)

            def split_max(s, r):
                if later(s, 2):
                    g.wait_ge(mt_ready, s - 1)
                g.wait_ge(max_done, NT * s + NT)
                hi, mid, lo = (mparts[:, r, n * NT:(n + 1) * NT] for n in range(PARTS))
                nc.gpsimd.tensor_tensor(hi, zeros[:, :], mx[:, r, :], ALU.subtract).then_inc(m_step, 1)
                g.wait_ge(m_step, 5 * s + 1)
                nc.gpsimd.tensor_tensor(mres[:, r, :], mx[:, r, :], hi, ALU.add).then_inc(m_step, 1)
                g.wait_ge(m_step, 5 * s + 2)
                nc.gpsimd.tensor_tensor(mid, zeros[:, :], mres[:, r, :], ALU.subtract).then_inc(m_step, 1)
                g.wait_ge(m_step, 5 * s + 3)
                nc.gpsimd.tensor_tensor(mlast[:, r, :], mres[:, r, :], mid, ALU.add).then_inc(m_step, 1)
                g.wait_ge(m_step, 5 * s + 4)
                nc.gpsimd.tensor_tensor(lo, zeros[:, :], mlast[:, r, :], ALU.subtract).then_inc(m_step, 1)

            split_max(0, 0)
            split_max(1, 1)

            def conv_taps(lo, hi):
                for k in range(lo, min(hi, POOL_TAPS[0])):
                    tap = PE_TAPS[0] + DVE_TAPS[0] + k
                    if k >= ALONE:
                        g.wait_ge(S("act_product", 0), k - ALONE + 1)
                        g.wait_ge(S("pool_tap", 0), k)
                        nc.gpsimd.tensor_tensor(acc_pool, acc_pool, products[(k - ALONE) % 2], ALU.add)\
                            .then_inc(S("pool_tap", 0), 1)
                        continue
                    if k == 0:
                        g.wait_ge(S("xpad", 0), 2)
                        nc.gpsimd.tensor_scalar(image(acc_pool), window(0, tap), weight(tap), 0.0, ALU.mult, ALU.add)\
                            .then_inc(S("pool_tap", 0), 1)
                    else:
                        g.wait_ge(S("pool_tap", 0), k)
                        nc.gpsimd.tensor_scalar(image(product), window(0, tap), weight(tap), 0.0, ALU.mult, ALU.add)\
                            .then_inc(S("pool_product"), 1)
                        g.wait_ge(S("pool_product"), k)
                        nc.gpsimd.tensor_tensor(acc_pool, acc_pool, product, ALU.add).then_inc(S("pool_tap", 0), 1)

            def add_products(h, lo, hi):
                for k in range(max(lo, 1), min(hi, POOL_TAPS[1])):
                    m = (POOL_TAPS[1] - 1) * h + k - 1
                    g.wait_ge(S("act_product", 1), POOL_TAPS[1] * h + k + 1)
                    if m:
                        g.wait_ge(S("pool_tap", 1), m)
                    half = acc_pool[:, h * HALF:(h + 1) * HALF]
                    nc.gpsimd.tensor_tensor(half, half, product[:, m % 2 * HALF:(m % 2 + 1) * HALF], ALU.add)\
                        .then_inc(S("pool_tap", 1), 1)

            def ln_pow(k):
                g.wait_ge(S("ln_ve"), k + 1)
                nc.gpsimd.tensor_tensor(rstd[:, k, 0:tiles(k)], vareps[:, k, 0:tiles(k)], power[:, 0:tiles(k)],
                                        ALU.pow).then_inc(S("ln_rstd"), 1)

            with g.Fori(1, (FINISH + 1) // 2 + 1) as pair:
                split_max(2 * pair, 0)
                split_max(2 * pair + 1, 1)
            gn_pool(g, B)
            split_max(FINISH + 3, 0)
            conv_taps(0, 2)
            for s in range(FINISH + 4, T):
                split_max(s, s % 2)
                conv_taps(3 * (s - FINISH - 4) + 2, 3 * (s - FINISH - 4) + 5)
            conv_taps(3 * (T - FINISH - 4) + 2, POOL_TAPS[0])
            ln_pow(0)
            gn_pool(g, B + 1)
            add_products(0, 0, POOL_TAPS[1])
            add_products(1, 0, 7)
            ln_pow(1)
            add_products(1, 7, POOL_TAPS[1])
            ln_pow(2)

        @block.scalar
        def _(a):
            a.wait_ge(S("power"), 2)
            nc.scalar.activation(loaded[:, :], zeros[:, 0:1], ACT.Exp).then_inc(S("loaded"), 1)
            a.wait_ge(S("w"), 16)
            a.wait_ge(S("va0"), 2)
            for b in range(B):
                for i in range(2):
                    a.wait_ge(S(f"proj{i}", b), 1)
                    if b:
                        a.wait_ge(S(f"sent{i}0", b - 1), 16)
                    nc.scalar.activation(part[:, i, 0, :], sm[i], ACT.Identity, bias=vec(V_BQ + i)).then_inc(S(f"part{i}0", b), 1)
                    if b:
                        a.wait_ge(S(f"part{i}2", b - 1), 1)
                        nc.scalar.activation(rest[:, i, :], sm[i], ACT.Identity, bias=vec(V_BQ + i))\
                            .then_inc(S(f"copied{i}"), 1)
                a.wait_ge(S("projv", b), 1)
                for c in range(2):
                    for j in range(4):
                        last = nc.scalar.activation(
                            va[:, :].rearrange("p (t j v) -> p j t v", j=NT, v=VW)
                            [:, 4 * c + j, b * HEADS:(b + 1) * HEADS, 0:D],
                            st[c][:, j * P:(j + 1) * P].rearrange("p (h d) -> p h d", d=D), ACT.Copy)
                last.then_inc(S("va", b), 1)

            def copy_max(s, r):
                a.wait_ge(mt_ready, s + 1)
                if later(s, 2):
                    a.wait_ge(s_mrow[r], (s - r) * 8)
                nc.scalar.activation(mrows[:, r, :], mt, ACT.Copy).then_inc(mt_done, 1)

            def copy_u(t, r):
                a.wait_ge(pv_done, NT * t + NT)
                if later(t, 2):
                    a.wait_ge(ot_ready, t - 1)
                nc.scalar.activation(u[:, r, :], pv[:, 0:2 * P], ACT.Copy).then_inc(u_ready, 1)

            def head(t, r, turn=LAG + 2, also={}):
                for j in range(NT):
                    for c in range(2):
                        a.wait_ge(st_ready, 2 * NT * t + (2 * j + c + 1))
                        if c == 0 and not (isinstance(t, int) and NT * t + j < PR):
                            a.wait_ge(pv_done, NT * t + (j - PR + 1))
                        nc.scalar.activation(pr[:, j % PR, c * HALF:(c + 1) * HALF], st[c], ACT.Exp,
                                             scale=SCALE).then_inc(exp_done, 1)
                    if j == 0 and later(t, 1):
                        copy_u(t - 1, 1 - r)
                    if j == turn:
                        copy_max(t + 1, 1 - r)
                    if j in also:
                        also[j]()

            def copy_oc():
                a.wait_ge(S("ot_T", 0), 1)
                nc.scalar.activation(oc[:, 0, :], sm[0], ACT.Copy).then_inc(S("oc", 0), 1)

            copy_max(0, 0)
            head(0, 0)
            head(1, 1)
            with a.Fori(1, FINISH // 2) as pair:
                head(2 * pair, 0)
                head(2 * pair + 1, 1)
            for t in range(FINISH - 1, T - 2):
                head(t, t % 2, turned(t), also={LAG: copy_oc} if t == FINISH else {})

            def ln_square(k):
                b, lo, hi = PIECES[k]
                a.wait_ge(S("centred"), k + 1)
                nc.scalar.activation(sq[b][:, lo:hi], centred[:, lo:hi], ACT.Square).then_inc(S("sq"), 1)
                nc.scalar.activation(yc[b][:, lo:hi], centred[:, lo:hi], ACT.Copy).then_inc(S("yc"), 1)

            def gelus(k, first=0, end=FC):
                b, lo, hi = PIECES[k]
                for f in range(first, end):
                    a.wait_ge(S("hid"), FC * k + f + 1)
                    a.wait_ge(S("b1"), 1)
                    nc.scalar.activation(hid[b][:, f, lo:hi], sm[f % 2][:, lo:hi], ACT.Gelu,
                                         bias=b1s[:, f:f + 1]).then_inc(S("gelu"), 1)

            def first_products(lo, hi):
                for m in range(lo, min(hi, POOL_TAPS[0] - ALONE)):
                    tap = PE_TAPS[0] + DVE_TAPS[0] + ALONE + m
                    a.wait_ge(S("xpad", 0), 2)
                    a.wait_ge(S("pool_tap", 0), ALONE + max(m - 1, 0))
                    nc.scalar.activation(image(products[m % 2]), window(0, tap), ACT.Copy, scale=weight(tap))\
                        .then_inc(S("act_product", 0), 1)

            def half_products(h, lo, hi):
                for k in range(lo, min(hi, POOL_TAPS[1])):
                    tap = PE_TAPS[1] + DVE_TAPS[1] + k
                    a.wait_ge(S("xpad", 1), 2)
                    a.wait_ge(S("acc"), 1)
                    if k == 0:
                        dest = acc_pool[:, h * HALF:(h + 1) * HALF]
                    else:
                        m = (POOL_TAPS[1] - 1) * h + k - 1
                        if m >= 2:
                            a.wait_ge(S("pool_tap", 1), m - 1)
                        dest = product[:, m % 2 * HALF:(m % 2 + 1) * HALF]
                    nc.scalar.activation(image(dest), window(1 + h, tap), ACT.Copy, scale=weight(tap))\
                        .then_inc(S("act_product", 1), 1)

            head(T - 2, 0, also={j: lambda m=j - 1: first_products(m, m + 1) for j in range(1, NT)})
            head(T - 1, 1, None, also={3: lambda: ln_square(0)})
            copy_u(T - 1, 1)
            a.wait_ge(S("ot_T", 1), 1)
            nc.scalar.activation(oc[:, 1, 0:HALF], lower[:, 0:HALF], ACT.Copy).then_inc(S("oc", 1), 1)
            gelus(0)
            half_products(0, 0, POOL_TAPS[1])
            half_products(1, 0, 5)
            ln_square(1)
            half_products(1, 5, POOL_TAPS[1])
            gelus(1, 0, 2)
            ln_square(2)
            gelus(1, 2)
            gelus(2)

        @block.vector
        def _(v):
            def split_rest(i):
                v.wait_ge(S(f"proj{i}", 0), 1)
                v.wait_ge(S(f"part{i}0", 0), 1)
                nc.vector.scalar_tensor_tensor(out=rest[:, i, :], in0=sm[i], scalar=vec(V_BQ + i),
                                               in1=part[:, i, 0, :], op0=ALU.add, op1=ALU.subtract)\
                    .then_inc(S(f"rest{i}", 0), 1)

            def split_copied(i):
                v.wait_ge(S(f"copied{i}"), 1)
                v.wait_ge(S(f"part{i}0", 1), 1)
                nc.vector.tensor_tensor(rest[:, i, :], rest[:, i, :], part[:, i, 0, :], ALU.subtract)\
                    .then_inc(S(f"rest{i}", 1), 1)

            def split_mid(b, i):
                v.wait_ge(S(f"rest{i}", b), 1)
                if b:
                    v.wait_ge(S(f"sent{i}1", b - 1), 16)
                nc.vector.tensor_copy(part[:, i, 1, :], rest[:, i, :]).then_inc(S(f"part{i}1", b), 1)

            def split_low(b, i):
                v.wait_ge(S(f"part{i}1", b), 1)
                if b:
                    v.wait_ge(S(f"sent{i}2", b - 1), 16)
                nc.vector.tensor_tensor(part[:, i, 2, :], rest[:, i, :], part[:, i, 1, :], ALU.subtract)\
                    .then_inc(S(f"part{i}2", b), 1)

            v.wait_ge(S("w"), 16)
            gn_stats(v, 0, xs[:, 0, :], lambda c: (S("x", 0), 16))
            gn_spread(v, 0)
            gn_vareps(v, 0)
            gn_apply(v, 0, xs[:, 0, :], xn[:, 0, :], S("xn", 0))
            gn_stats(v, 1, xs[:, 1, :], lambda c: (S("x", 1), 16))
            gn_spread(v, 1)
            split_rest(0)
            gn_vareps(v, 1)
            split_rest(1)
            for i in range(2):
                split_mid(0, i)
            gn_apply(v, 1, xs[:, 1, :], xn[:, 1, :], S("xn", 1))
            for i in range(2):
                split_low(0, i)
            for i in range(2):
                split_copied(i)
                split_mid(1, i)

            def maxima(s, r, i):
                v.wait_ge(s_ready, NT * s + (i + 1))
                if i == 0 and later(s, 2):
                    v.wait_ge(m_step, 5 * s - 5)
                nc.vector.tensor_reduce(mx[:, r, i:i + 1], sm[i % 2], AX.X, ALU.max).then_inc(max_done, 1)

            def normalise(t, r):
                v.wait_ge(ot_ready, t + 1)
                nc.vector.reciprocal(rden[:, r, :, :], otp[:, :, :, D]).then_inc(rd_ready, 1)
                v.wait_ge(rd_ready, t + 1)
                nc.vector.tensor_tensor(
                    ot[:, :, bass.ds(t * D, D)].rearrange("p (q k) d -> p q k d", k=2),
                    otp[:, :, :, 0:D],
                    rden[:, r, :, :].rearrange("p q (k a) -> p q k a", a=1).broadcast_to([P, 4, 2, D]), ALU.mult).then_inc(ot_done, 1)

            def head(t, r, also={}):
                for i in range(NT):
                    if isinstance(t, int):
                        for s, n in plan[t][i]:
                            maxima(s, s % 2, n)
                    elif i < LAG:
                        maxima(t + 1, 1 - r, NT - LAG + i)
                    else:
                        maxima(t + 2, r, i - LAG)
                    if i == 3 and later(t, 1):
                        normalise(t - 1, 1 - r)
                    if i in also:
                        also[i]()

            def residual():
                v.wait_ge(S("projp", 0), 1)
                nc.vector.scalar_tensor_tensor(out=x1[:, 0, :], in0=sm[1], scalar=vec(V_BP), in1=xs[:, 0, :],
                                               op0=ALU.add, op1=ALU.add).then_inc(S("x1", 0), 1)

            inner = xpad[:, 0:PADDED].rearrange("p (a c) -> p a c", c=WIDE)[:, PAD:PAD + SIDE, PAD:PAD + SIDE]

            def conv_taps(k, lo, hi=None):
                b, first, end = PIECES[k]
                before = DVE_TAPS[b] * (k - b)
                sums = image(acc[b][:, first:end])
                for n in range(lo, DVE_TAPS[b] if hi is None else min(hi, DVE_TAPS[b])):
                    tap = PE_TAPS[b] + n
                    if n == 0:
                        v.wait_ge(S("xpad", b), 2)
                        if b == 0:
                            v.wait_ge(st_ready, 2 * NT * (HEADS + 1))
                        nc.vector.tensor_scalar(sums, window(k, tap), weight(tap), vec(V_CB), ALU.mult, ALU.add)\
                            .then_inc(S("dve_tap", b), 1)
                    else:
                        v.wait_ge(S("dve_tap", b), before + n)
                        nc.vector.scalar_tensor_tensor(out=sums, in0=window(k, tap), scalar=weight(tap), in1=sums,
                                                       op0=ALU.mult, op1=ALU.add).then_inc(S("dve_tap", b), 1)

            def conv_sum(k):
                b, lo, hi = PIECES[k]
                v.wait_ge(S("dve_tap", b), DVE_TAPS[b] * (k - b + 1))
                v.wait_ge(S("pool_tap", b), (POOL_TAPS[b] - b) * (k - b + 1))
                nc.vector.tensor_tensor(acc[b][:, lo:hi], acc[b][:, lo:hi], acc_pool[:, lo:hi], ALU.add)\
                    .then_inc(S("acc"), 1)
                v.wait_ge(S("acc"), k + 1)
                v.wait_ge(S(f"conv{lo // HALF}", b), 1)
                v.wait_ge(S(f"conv{hi // HALF - 1}", b), 1)
                nc.vector.tensor_tensor(y[b][:, lo:hi], conv_out[:, lo:hi], acc[b][:, lo:hi], ALU.add)\
                    .then_inc(S("y"), 1)

            def ln_copy(k):
                v.wait_ge(S("ln_var"), k + 1)
                nc.vector.tensor_copy(variance[:, k, 0:quarter(k)], var_out(k)).then_inc(S("ln_row"), 1)

            def ln_eps(k):
                v.wait_ge(S("ln_turned"), k + 1)
                nc.vector.tensor_scalar(vareps[:, k, 0:tiles(k)], var_turned(k), LN_EPS, None, ALU.add)\
                    .then_inc(S("ln_ve"), 1)

            def ln_diag(k):
                v.wait_ge(S("ln_rstd"), k + 1)
                if k:
                    v.wait_ge(S("scale"), k)
                nc.vector.tensor_tensor(
                    diag[:, 0:tiles(k) * P].rearrange("p (i c) -> p i c", c=P),
                    ident.rearrange("p (a c) -> p a c", a=1).broadcast_to([P, tiles(k), P]),
                    rstd[:, k, 0:tiles(k)].rearrange("p (i a) -> p i a", a=1).broadcast_to([P, tiles(k), P]), ALU.mult)\
                    .then_inc(S("diag"), 1)

            def ln_apply(k):
                b, lo, hi = PIECES[k]
                v.wait_ge(S("scale"), k + 1)
                v.wait_ge(S("yc"), k + 1)
                nc.vector.tensor_tensor(yn[:, b, lo:hi], yc[b][:, lo:hi], scale_out(k)[:, 0:hi - lo], ALU.mult)\
                    .then_inc(S("yn"), 1)

            def output(k):
                b, lo, hi = PIECES[k]
                v.wait_ge(S("mlp"), k + 1)
                nc.vector.scalar_tensor_tensor(out=fin[b][:, lo:hi], in0=mlp_out[:, lo:hi], scalar=vec(V_B2),
                                               in1=x1[:, b, lo:hi], op0=ALU.add, op1=ALU.add).then_inc(S("fin"), 1)

            for s, i in first_tiles:
                maxima(s, s, i)
            head(0, 0, {4: lambda: split_low(1, 0)})
            head(1, 1, {4: lambda: split_low(1, 1)})
            with v.Fori(1, FINISH // 2) as pair:
                head(2 * pair, 0)
                head(2 * pair + 1, 1)

            def apply_mid():
                v.wait_ge(S("xpad0"), 1)
                gn_apply(v, B, x1[:, 0, :], inner, S("xpad", 0))

            also = {FINISH: {LAG + 1: residual},
                    FINISH + 1: {4: lambda: gn_stats(v, B, x1[:, 0, :], lambda c: (S("x1", 0), 1))},
                    FINISH + 2: {0: lambda: gn_spread(v, B), 2: lambda: gn_vareps(v, B), 4: apply_mid}}
            for t in range(FINISH - 1, T - 2):
                head(t, t % 2, also.get(t, {}))
            v.wait_ge(S("w12"), 32)
            nc.vector.tensor_scalar(w1g[:, :], w1s[:, :], vec(V_G), None, ALU.mult).then_inc(S("w1g"), 1)
            conv_taps(0, 0, 3)
            v.wait_ge(S("lnb"), 1)
            nc.vector.tensor_tensor(b1s[:, :], sm[1][:, 0:FC], vec(V_B1, FC), ALU.add).then_inc(S("b1"), 1)
            conv_taps(0, 3, 5)
            normalise(T - 3, 1)
            conv_taps(0, 5)
            conv_sum(0)
            normalise(T - 2, 0)
            ln_copy(0)
            ln_eps(0)
            ln_diag(0)
            ln_apply(0)
            normalise(T - 1, 1)
            v.wait_ge(S("ot_T", 1), 2)
            nc.vector.tensor_copy(oc[:, 1, HALF:N], lower[:, HALF:N]).then_inc(S("oc_low"), 1)
            for c in range(2):
                v.wait_ge(S("projp", 1), c + 1)
                cols = slice(c * HALF, (c + 1) * HALF)
                nc.vector.scalar_tensor_tensor(out=x1[:, 1, cols], in0=lower[:, cols], scalar=vec(V_BP),
                                               in1=xs[:, 1, cols], op0=ALU.add, op1=ALU.add).then_inc(S("x1", 1), 1)
            gn_stats(v, B + 1, x1[:, 1, :], lambda c: (S("x1", 1), c + 1))
            gn_spread(v, B + 1)
            gn_vareps(v, B + 1)
            for h in range(2):
                v.wait_ge(S(f"pad_sent{h}", 0), 16)
            v.wait_ge(S("pool_tap", 0), POOL_TAPS[0])
            gn_apply(v, B + 1, x1[:, 1, :], inner, S("xpad", 1))
            conv_taps(1, 0)
            output(0)
            conv_taps(2, 0, 3)
            conv_sum(1)
            conv_taps(2, 3, 7)
            ln_copy(1)
            conv_taps(2, 7, 8)
            ln_eps(1)
            conv_taps(2, 8, 10)
            ln_diag(1)
            conv_taps(2, 10)
            ln_apply(1)
            conv_sum(2)
            ln_copy(2)
            ln_eps(2)
            ln_diag(2)
            ln_apply(2)
            output(1)
            output(2)

        @block.tensor
        def _(t_):
            def project(b, i):
                t_.wait_ge(S("xn", b), 1)
                if b:
                    t_.wait_ge(S(f"part{i}0", b - 1), 1)
                    t_.wait_ge(S(f"rest{i}", b - 1), 1)
                for c in range(2):
                    last = nc.tensor.matmul(sm[i][:, c * HALF:(c + 1) * HALF], vec(C_WQ + i * P, P),
                                            xn[:, b, c * HALF:(c + 1) * HALF], start=True, stop=True)
                last.then_inc(S(f"proj{i}", b), 1)

            def project_v(b):
                t_.wait_ge(S("bv"), 16)
                if b:
                    t_.wait_ge(S("va", b - 1), 1)
                for j in range(NT):
                    o = st[j // 4][:, (j % 4) * P:(j % 4 + 1) * P]
                    nc.tensor.matmul(o, xn[:, b, j * P:(j + 1) * P], vec(C_WV, P), start=True, stop=False)
                    last = nc.tensor.matmul(o, ones[0:1, :], bv[:, :], start=False, stop=True)
                last.then_inc(S("projv", b), 1)

            def keep_busy(n):
                for _ in range(n):
                    nc.tensor.matmul(pv, warm[:, 0:P], warm[:, :], start=True, stop=True)

            t_.wait_ge(S("warm"), 1)
            keep_busy(14)
            t_.wait_ge(S("w"), 16)
            gn_pe_mean(t_, 0)
            gn_pe_var(t_, 0)
            keep_busy(8)
            project(0, 0)
            gn_pe_mean(t_, 1)
            project(0, 1)
            gn_pe_var(t_, 1)
            project_v(0)
            project(1, 0)
            project(1, 1)
            project_v(1)

            def scores(s, i):
                if NT * s + i >= 2:
                    t_.wait_ge(max_done, NT * s + (i - 1))
                if (s, i) == (FINISH + 2, 0):
                    t_.wait_ge(S("oc", 0), 1)
                if (s, i) == (FINISH + 2, 1):
                    t_.wait_ge(S("x1", 0), 1)
                for c in range(2):
                    last = nc.tensor.matmul(sm[i % 2][:, c * HALF:(c + 1) * HALF],
                                            qs[0:STACK, bass.ds(s * N + i * P, P)],
                                            ks[0:STACK, bass.ds(s * N + c * HALF, HALF)], start=True, stop=True)
                last.then_inc(s_ready, 1)

            def turn_max(s, r):
                t_.wait_ge(m_step, 5 * s + 5)
                if later(s, 1):
                    t_.wait_ge(mt_done, s)
                if later(s, 2):
                    t_.wait_ge(ot_done, s - 1)
                nc.tensor.transpose(mt, mparts[:, r, :], idb[:, :]).then_inc(mt_ready, 1)

            def turn_u(t, r):
                t_.wait_ge(u_ready, t + 1)
                t_.wait_ge(mt_done, min(t + 2, T))
                if t == FINISH + 1:
                    t_.wait_ge(S("gn_ve"), B + 1)
                if later(t, 1):
                    t_.wait_ge(ot_done, t)
                for i in range(2):
                    last = nc.tensor.transpose(mi[:, OT_AT + i * P:OT_AT + (i + 1) * P],
                                               u[:, r, i * P:(i + 1) * P], ident)
                last.then_inc(ot_ready, 1)

            def scores_t(t, j):
                for c in range(2):
                    if not (isinstance(t, int) and 2 * NT * t + 2 * j + c < 2):
                        t_.wait_ge(exp_done, 2 * NT * t + (2 * j + c - 1))
                    nc.tensor.matmul(st[c], ks[0:ROWS, bass.ds(t * N + j * P, P)],
                                     qs[0:ROWS, bass.ds(t * N + c * HALF, HALF)],
                                     start=True, stop=True).then_inc(st_ready, 1)

            def times_v(t, r, j):
                if j == 0:
                    if later(t, 1):
                        t_.wait_ge(u_ready, t)
                t_.wait_ge(exp_done, 2 * NT * t + (2 * j + 2))
                for q in range(4):
                    last = nc.tensor.matmul(pv[q * VW:(q + 1) * VW, 0:2 * P], va[:, (t * NT + j) * VW:(t * NT + j + 1) * VW],
                                            pr[:, j % PR, 2 * P * q:2 * P * (q + 1)],
                                            start=(j == 0), stop=(j == NT - 1))
                last.then_inc(pv_done, 1)

            def head(t, r, turn=LAG + 2, also=()):
                for j in range(NT):
                    if j == 0:
                        t_.wait_ge(s_mrow[r], (t - r) * 8 + 16)
                    scores_t(t, j)
                    if j:
                        times_v(t, r, j - 1)
                    elif t:
                        times_v(t - 1, 1 - r, NT - 1)
                    if j == turn:
                        turn_max(t + 1, 1 - r)
                    if j == 3 and t:
                        turn_u(t - 1, 1 - r)
                    for step, function, *given in also:
                        if step == j:
                            function(*given)
                    for s, i in plan[t][j]:
                        scores(s, i)

            def finish_turn():
                t_.wait_ge(ot_done, HEADS)
                t_.wait_ge(max_done, NT * (FINISH + 2) - 1)
                for i in range(NT):
                    last = nc.tensor.transpose(sm[0][:, i * P:(i + 1) * P], ot[:, i, 0:P], ident)
                last.then_inc(S("ot_T", 0), 1)

            def finish_project():
                t_.wait_ge(S("oc", 0), 1)
                t_.wait_ge(max_done, NT * (FINISH + 2))
                for c in range(2):
                    last = nc.tensor.matmul(sm[1][:, c * HALF:(c + 1) * HALF], vec(C_WP, P),
                                            oc[:, 0, c * HALF:(c + 1) * HALF], start=True, stop=True)
                last.then_inc(S("projp", 0), 1)

            def mid_mean():
                t_.wait_ge(mt_done, FINISH + 3)
                t_.wait_ge(ot_done, FINISH + 1)
                gn_pe_mean(t_, B)

            for i in range(2):
                t_.wait_ge(S(f"copied{i}"), 1)
                t_.wait_ge(S(f"part{i}0", 1), 1)
            t_.wait_ge(S("stack_first"), 16 * 12)
            t_.wait_ge(S("idb"), 1)
            for s, i in first_tiles:
                scores(s, i)
                if (s, i) == (1, 2):
                    turn_max(0, 0)
            t_.wait_ge(S("kones"), 16)
            t_.wait_ge(S("va", 1), 1)
            also = {FINISH: [(LAG, finish_turn), (LAG + 2, finish_project)],
                    FINISH + 2: [(0, mid_mean), (2, gn_pe_var, t_, B)]}
            for t in range(T - 2):
                if t == 0:
                    t_.wait_ge(S("stack", 0), 16 * 12)
                if t == HEADS - 3:
                    t_.wait_ge(S("stack", 1), 16 * 12)
                head(t, t % 2, turned(t), also.get(t, ()))

            def conv(b, half, lo, hi):
                if lo == 0:
                    t_.wait_ge(S(f"rep{half}", b), 16 * SHIFTS)
                for m in range(lo, hi):
                    dy, e = m // SPAN, m % SPAN
                    at = (dy + half * SIDE // 2) * WIDE + e * SHIFTS
                    for g in range(GROUPS):
                        rows = xr[:, g, at:at + SIDE // 2 * WIDE].rearrange("p (a c) -> p a c", c=WIDE)
                        last = nc.tensor.matmul(conv_out[g * CG:(g + 1) * CG, half * HALF:(half + 1) * HALF],
                                                wt[:, g * KS * SPAN + m, :], rows[:, :, 0:SIDE],
                                                start=(m == 0), stop=(m == PE_RUNS[b] - 1))
                if hi == PE_RUNS[b]:
                    last.then_inc(S(f"conv{half}", b), 1)

            def first_bias():
                t_.wait_ge(S("w12"), 32)
                t_.wait_ge(S("wt"), 1)
                t_.wait_ge(max_done, NT * T)
                for f in range(FC):
                    last = nc.tensor.matmul(sm[1][:, f:f + 1], w1s[:, f * P:(f + 1) * P], vec(V_B), start=True, stop=True)
                last.then_inc(S("lnb"), 1)

            def banks(k):
                _, lo, hi = PIECES[k]
                return [slice(c, c + HALF) for c in range(lo, hi, HALF)]

            def centre_out(k):
                b = PIECES[k][0]
                t_.wait_ge(S("y"), k + 1)
                t_.wait_ge(S("b1"), 1)
                for cols in banks(k):
                    last = nc.tensor.matmul(centred[:, cols], centre, y[b][:, cols], start=True, stop=True)
                last.then_inc(S("centred"), 1)

            def ln_var(k):
                b, lo, _ = PIECES[k]
                t_.wait_ge(S("sq"), k + 1)
                if k == 2:
                    t_.wait_ge(S("ln_ve"), 2)
                for q in range(4):
                    last = nc.tensor.matmul(var_out(k)[q * VW:(q + 1) * VW, :], w[:, C_MEAN:C_MEAN + VW],
                                            sq[b][:, lo + q * quarter(k):lo + (q + 1) * quarter(k)],
                                            start=True, stop=True)
                last.then_inc(S("ln_var"), 1)

            def ln_turn(k):
                t_.wait_ge(S("ln_row"), k + 1)
                for n in range(quarter(k) // P):
                    last = nc.tensor.matmul(var_turned(k).rearrange("p (q n) -> p q n", n=quarter(k) // P)[:, :, n],
                                            variance[:, k, n * P:(n + 1) * P], ident[:, 0:P:VW],
                                            start=True, stop=True)
                last.then_inc(S("ln_turned"), 1)

            def ln_scale(k):
                t_.wait_ge(S("diag"), k + 1)
                t_.wait_ge(*((S("yn"), 2) if k == 2 else (S("yc"), k + 1)))
                for c in range(len(banks(k))):
                    last = nc.tensor.matmul(scale_out(k)[:, c * HALF:(c + 1) * HALF], ones,
                                            diag[:, c * HALF:(c + 1) * HALF], start=True, stop=True)
                last.then_inc(S("scale"), 1)

            def mlp(k, f, c=None):
                b = PIECES[k][0]
                if f == 0:
                    t_.wait_ge(S("yn"), k + 1)
                    t_.wait_ge(S("w1g"), 1)
                elif f >= 2:
                    t_.wait_ge(S("gelu"), FC * k + f - 1)
                for n, cols in enumerate(banks(k)):
                    if c is None or c == n:
                        last = nc.tensor.matmul(sm[f % 2][:, cols], w1g[:, f * P:(f + 1) * P],
                                                yn[:, b, cols], start=True, stop=True)
                if c != 0:
                    last.then_inc(S("hid"), 1)

            def mlp_down(k, f):
                b = PIECES[k][0]
                t_.wait_ge(S("gelu"), FC * k + f + 1)
                if f == 0:
                    if k:
                        t_.wait_ge(S("fin"), 1)
                    else:
                        t_.wait_ge(S("x1", 1), 2)
                for cols in banks(k):
                    last = nc.tensor.matmul(mlp_out[:, cols], w2s[:, f, :], hid[b][:, f, cols],
                                            start=(f == 0), stop=(f == FC - 1), skip_group_check=True)
                if f == FC - 1:
                    last.then_inc(S("mlp"), 1)

            units = PE_RUNS[0]
            head(T - 2, 0, also=[(0, first_bias)]
                 + [(1 + n * 7 // (2 * units), conv, 0, n // units, n % units, n % units + 1) for n in range(2 * units)])
            head(T - 1, 1, None,
                 also=[(2, centre_out, 0), (3, ln_var, 0), (4, ln_turn, 0), (7, ln_scale, 0)])
            times_v(T - 1, 1, NT - 1)
            turn_u(T - 1, 1)
            mlp(0, 0, 0)
            t_.wait_ge(ot_done, T)
            for i in range(NT):
                last = nc.tensor.transpose(lower[:, i * P:(i + 1) * P], ot[:, i, P:2 * P], ident)
                if i % (NT // 2) == NT // 2 - 1:
                    last.then_inc(S("ot_T", 1), 1)
            mlp(0, 0, 1)
            for c, done in enumerate((S("oc", 1), S("oc_low"))):
                t_.wait_ge(done, 1)
                nc.tensor.matmul(lower[:, c * HALF:(c + 1) * HALF], vec(C_WP, P), oc[:, 1, c * HALF:(c + 1) * HALF],
                                 start=True, stop=True).then_inc(S("projp", 1), 1)
            mlp(0, 1)
            mlp(0, 2, 0)
            gn_pe_mean(t_, B + 1)
            mlp(0, 2, 1)
            gn_pe_var(t_, B + 1)
            mlp(0, 3)
            for f in range(FC):
                mlp_down(0, f)
            units = PE_RUNS[1]
            conv(1, 0, 0, units)
            conv(1, 1, 0, 1)
            centre_out(1)
            conv(1, 1, 1, 3)
            ln_var(1)
            conv(1, 1, 3, 4)
            ln_turn(1)
            conv(1, 1, 4, 7)
            ln_scale(1)
            conv(1, 1, 7, units)
            mlp(1, 0)
            mlp(1, 1)
            centre_out(2)
            mlp(1, 2)
            ln_var(2)
            mlp(1, 3)
            ln_turn(2)
            for f in range(0, FC - 1):
                mlp_down(1, f)
            ln_scale(2)
            for f in range(FC - 1, FC):
                mlp_down(1, f)
            mlp(2, 0)
            mlp(2, 1)
            for f in range(2, FC):
                mlp(2, f)
                mlp_down(2, f - 2)
            for f in range(2, FC):
                mlp_down(2, f)
    return nc


def kernel(**inputs):
    import numpy as np
    import concourse.bacc as bacc
    from concourse.bass_utils import run_bass_kernel_spmd

    def get(name):
        return np.ascontiguousarray(inputs[name])

    def heads_on_diagonal(m):
        full = np.zeros((P, P), m.dtype)
        for h in range(HEADS):
            full[h * D:(h + 1) * D, h * D:(h + 1) * D] = m[h].T
        return full

    f32 = np.float32
    eye = np.eye(P, dtype=f32)
    centre = (eye - np.full((P, P), 1.0 / P, f32)).astype(f32)
    in_group = np.kron(np.eye(P // 4, dtype=f32), np.full((4, 4), 0.25, f32))
    mask = np.tile(np.eye(CG, dtype=f32), (SHIFTS, 1))
    conv_w = get("L1_conv_conv_w").reshape(P, KS, KS)
    taps = np.zeros((SHIFTS, CG, GROUPS, KS, SPAN), conv_w.dtype)
    for s in range(SHIFTS):
        for e in range(SPAN):
            if e * SHIFTS + s < KS:
                taps[s, :, :, :, e] = conv_w[:, :, e * SHIFTS + s].reshape(GROUPS, CG, KS).transpose(1, 0, 2)
    columns = [get(n).reshape(P, 1) for n in ("L0_conv_bq", "L0_conv_bk", "L0_conv_bp", "L1_conv_conv_b",
                                              "L1_conv_ln_g", "L1_conv_ln_b", "L1_conv_b2")]
    wpack = np.concatenate(
        [heads_on_diagonal(get(f"L0_conv_W{n}")) for n in "qkvp"]
        + [eye, centre, in_group, np.full((P, P), 1.0 / P, f32), np.ones((P, P), f32), mask,
           taps.reshape(P, TAPS), conv_w.reshape(P, KS * KS)]
        + columns + [get("L1_conv_b1").reshape(FC, P).T], axis=1)

    arrays = {
        "x": get("x").reshape(B, P, N),
        "wpack": np.ascontiguousarray(wpack),
        "bvrow": get("L0_conv_bv").reshape(1, P),
        "ones3": np.ones((PARTS, T * N), mybir.dt.np(BF16)),
        "w1": get("L1_conv_w1"),
        "w2": get("L1_conv_w2"),
    }
    nc = bacc.Bacc("TRN2", target_bir_lowering=False, num_devices=1)
    args = [nc.dram_tensor(n, a.shape, mybir.dt.from_np(a.dtype), kind="ExternalInput").ap()
            for n, a in arrays.items()]
    out = nc.dram_tensor("out", (B, P, N), F32, kind="ExternalOutput").ap()
    build(nc, *args, out)
    r = run_bass_kernel_spmd(nc, [arrays], core_ids=[0])
    return r.results[0]["out"].reshape(B, P, SIDE, SIDE)
```
